# Optimizing a Trainium2 kernel written in Bass

```python
import numpy as np
import jax
import jax.numpy as jnp

def _softmax(x, axis=-1):
    return jax.nn.softmax(x, axis=axis)

def _gelu(x):
    return jax.nn.gelu(x, approximate=True)

def _silu(x):
    return jax.nn.silu(x)

def _sigmoid(x):
    return jax.nn.sigmoid(x)

def _layernorm(x, axis=-1, eps=1e-05):
    m = jnp.mean(x, axis=axis, keepdims=True)
    v = jnp.var(x, axis=axis, keepdims=True)
    return (x - m) / jnp.sqrt(v + eps)

def _scatter_add(tgt, idx, src, axis=0):
    return tgt.at[idx].add(src)

def _segment_sum(src, seg, n):
    return jax.ops.segment_sum(src, seg, n)
kernel_name = 'mk_conv_attn_hybrid_d2_conv_nchw128_r4_dfda26'

def setup_inputs(seed: int=0):
    np.random.seed(seed)
    _w = jnp.asarray

    def _rec_inputs():
        import jax
        import jax.numpy as jnp
        _gk = jax.random.key(seed)
        x = -0.0005207 + 1.001 * jax.random.normal(jax.random.fold_in(_gk, 1), (4, 32, 16, 16), jnp.float32)
        return x
    x = _rec_inputs()

    def _L0_conv_setup():
        import jax, jax.numpy as jnp
        import numpy as np
        EPS = 1e-05

        def instance_norm(x, gamma, beta):
            mu = jnp.mean(x, axis=(2, 3), keepdims=True)
            var = jnp.var(x, axis=(2, 3), keepdims=True)
            xh = (x - mu) * jax.lax.rsqrt(var + EPS)
            return xh * gamma[None, :, None, None] + beta[None, :, None, None]

        def conv1x1(x, w, b):
            return jnp.einsum('bchw,oc->bohw', x, w) + b[None, :, None, None]
        key = jax.random.key(seed)
        ks = jax.random.split(key, 16)
        B, C, H, W = (4, 32, 16, 16)
        s = 1.0 / np.sqrt(C)
        inp = {'x': jax.random.normal(ks[0], (B, C, H, W), jnp.float32), 'in_gamma': jnp.ones((C,), jnp.float32), 'in_beta': jnp.zeros((C,), jnp.float32), 'wq': jax.random.uniform(ks[1], (C, C), jnp.float32, -s, s), 'bq': jax.random.uniform(ks[2], (C,), jnp.float32, -s, s), 'wk': jax.random.uniform(ks[3], (C, C), jnp.float32, -s, s), 'bk': jax.random.uniform(ks[4], (C,), jnp.float32, -s, s), 'wv': jax.random.uniform(ks[5], (C, C), jnp.float32, -s, s), 'bv': jax.random.uniform(ks[6], (C,), jnp.float32, -s, s), 'wo': jax.random.uniform(ks[7], (C, C), jnp.float32, -s, s), 'bo': jax.random.uniform(ks[8], (C,), jnp.float32, -s, s), 'w_cbr': jax.random.uniform(ks[9], (C, C), jnp.float32, -s, s), 'b_cbr': jax.random.uniform(ks[10], (C,), jnp.float32, -s, s), 'g_cbr': jnp.ones((C,), jnp.float32), 'be_cbr': jnp.zeros((C,), jnp.float32)}
        return inp
    _L0_conv_all = _L0_conv_setup()
    _L0_conv_in = {k: v for k, v in _L0_conv_all.items() if k in ('in_gamma', 'in_beta', 'wq', 'bq', 'wk', 'bk', 'wv', 'bv', 'wo', 'bo', 'w_cbr', 'b_cbr', 'g_cbr', 'be_cbr')}
    del _L0_conv_all

    def _L1_attn_setup():
        import jax, jax.numpy as jnp
        import numpy as np
        key = jax.random.key(seed)
        x = jax.random.normal(key, (4, 1024, 32), dtype=jnp.float32)
        return {'x': x}
    _L1_attn_all = _L1_attn_setup()
    _L1_attn_in = {k: v for k, v in _L1_attn_all.items() if k in ()}
    del _L1_attn_all

    def _L1_ffn_setup():
        import jax, jax.numpy as jnp
        import numpy as np
        B, S, D, E, H, O, K = (128, 512, 32, 16, 128, 32, 8)
        key = jax.random.key(seed)
        k0, k1, k2, k3 = jax.random.split(key, 4)
        x = jax.random.normal(k0, (B, S, D), dtype=jnp.float32)
        gate_w = jax.random.normal(k1, (E, D), dtype=jnp.float32) * (1.0 / np.sqrt(D))
        gate_b = jnp.zeros((E,), dtype=jnp.float32)
        weight1 = jax.random.uniform(k2, (E, D + 1, H), dtype=jnp.float32, minval=-1.0, maxval=1.0) * (1.0 / np.sqrt(D + 1))
        weight2 = jax.random.uniform(k3, (E, H + 1, O), dtype=jnp.float32, minval=-1.0, maxval=1.0) * (1.0 / np.sqrt(H + 1))
        return {'x': x, 'gate_w': gate_w, 'gate_b': gate_b, 'weight1': weight1, 'weight2': weight2}
    _L1_ffn_all = _L1_ffn_setup()
    _L1_ffn_in = {k: v for k, v in _L1_ffn_all.items() if k in ('gate_w', 'gate_b', 'weight1', 'weight2')}
    del _L1_ffn_all
    return {'x': x, 'L0_conv_in_gamma': _L0_conv_in['in_gamma'], 'L0_conv_in_beta': _L0_conv_in['in_beta'], 'L0_conv_wq': _L0_conv_in['wq'], 'L0_conv_bq': _L0_conv_in['bq'], 'L0_conv_wk': _L0_conv_in['wk'], 'L0_conv_bk': _L0_conv_in['bk'], 'L0_conv_wv': _L0_conv_in['wv'], 'L0_conv_bv': _L0_conv_in['bv'], 'L0_conv_wo': _L0_conv_in['wo'], 'L0_conv_bo': _L0_conv_in['bo'], 'L0_conv_w_cbr': _L0_conv_in['w_cbr'], 'L0_conv_b_cbr': _L0_conv_in['b_cbr'], 'L0_conv_g_cbr': _L0_conv_in['g_cbr'], 'L0_conv_be_cbr': _L0_conv_in['be_cbr'], 'L1_ffn_gate_w': _L1_ffn_in['gate_w'], 'L1_ffn_gate_b': _L1_ffn_in['gate_b'], 'L1_ffn_weight1': _L1_ffn_in['weight1'], 'L1_ffn_weight2': _L1_ffn_in['weight2']}

def reference(x, L0_conv_in_gamma, L0_conv_in_beta, L0_conv_wq, L0_conv_bq, L0_conv_wk, L0_conv_bk, L0_conv_wv, L0_conv_bv, L0_conv_wo, L0_conv_bo, L0_conv_w_cbr, L0_conv_b_cbr, L0_conv_g_cbr, L0_conv_be_cbr, L1_ffn_gate_w, L1_ffn_gate_b, L1_ffn_weight1, L1_ffn_weight2):
    import jax
    import jax.numpy as jnp

    def _L0_conv_ref(x, in_gamma, in_beta, wq, bq, wk, bk, wv, bv, wo, bo, w_cbr, b_cbr, g_cbr, be_cbr):
        import jax, jax.numpy as jnp
        import numpy as np
        EPS = 1e-05

        def instance_norm(x, gamma, beta):
            mu = jnp.mean(x, axis=(2, 3), keepdims=True)
            var = jnp.var(x, axis=(2, 3), keepdims=True)
            xh = (x - mu) * jax.lax.rsqrt(var + EPS)
            return xh * gamma[None, :, None, None] + beta[None, :, None, None]

        def conv1x1(x, w, b):
            return jnp.einsum('bchw,oc->bohw', x, w) + b[None, :, None, None]
        B, C, H, W = x.shape
        x_norm = instance_norm(x, in_gamma, in_beta)
        q = conv1x1(x_norm, wq, bq)
        k = conv1x1(x_norm, wk, bk)
        v = conv1x1(x_norm, wv, bv)
        N = H * W
        q = q.reshape(B, C, N).transpose(0, 2, 1)
        k = k.reshape(B, C, N)
        v = v.reshape(B, C, N).transpose(0, 2, 1)
        attn = jnp.einsum('bnc,bcm->bnm', q, k) * C ** (-0.5)
        attn = jax.nn.softmax(attn, axis=-1)
        o = jnp.einsum('bnm,bmc->bnc', attn, v)
        o = o.transpose(0, 2, 1).reshape(B, C, H, W)
        o = conv1x1(o, wo, bo)
        o = o + x
        cbr = jax.nn.relu(instance_norm(conv1x1(o, w_cbr, b_cbr), g_cbr, be_cbr))
        return o + cbr

    def _L1_attn_ref(x):
        import jax, jax.numpy as jnp
        import numpy as np
        scores = jnp.einsum('btd,bsd->bts', x, x)
        out = jnp.einsum('bts,bsd->btd', scores, x)
        return out

    def _L1_ffn_ref(x, gate_w, gate_b, weight1, weight2):
        import jax, jax.numpy as jnp
        import numpy as np
        B, S, D, E, H, O, K = (128, 512, 32, 16, 128, 32, 8)
        Bn, Sn, Dn = x.shape
        logits = jnp.einsum('bsd,ed->bse', x, gate_w) + gate_b
        probs = jax.nn.softmax(logits, axis=1)
        vals, idx = jax.lax.top_k(probs.transpose(0, 2, 1), K)
        topv = vals.transpose(0, 2, 1)
        topi = idx.transpose(0, 2, 1)
        flat_idx = topi.reshape(Bn, K * E)
        gathered = jnp.take_along_axis(x, flat_idx[:, :, None], axis=1)
        gathered = gathered.reshape(Bn, K, E, Dn)
        pooled = jnp.einsum('bked,bke->bed', gathered, topv)
        ones = jnp.ones((E, Bn, 1), dtype=x.dtype)
        h = jnp.concatenate([pooled.transpose(1, 0, 2), ones], axis=-1)
        h = jax.nn.gelu(jnp.einsum('ebd,edh->ebh', h, weight1), approximate=False)
        h = jnp.concatenate([h, ones], axis=-1)
        out = jnp.einsum('ebh,eho->ebo', h, weight2)
        out = out.transpose(1, 0, 2)
        weighted = jnp.einsum('beo,bke->bkeo', out, topv).reshape(Bn, K * E, O)
        outputs = jnp.zeros((Bn, Sn, O), dtype=x.dtype)
        outputs = outputs.at[jnp.arange(Bn)[:, None], flat_idx].add(weighted)
        return outputs

    def _gn(v, G=32, eps=1e-05):
        B_, C_, H_, W_ = v.shape
        g = v.reshape(B_, G, C_ // G, H_, W_)
        m = jnp.mean(g, axis=(2, 3, 4), keepdims=True)
        s = jnp.var(g, axis=(2, 3, 4), keepdims=True)
        return ((g - m) / jnp.sqrt(s + eps)).reshape(v.shape)

    def _ln_c(v, eps=1e-06):
        m = jnp.mean(v, axis=1, keepdims=True)
        s = jnp.var(v, axis=1, keepdims=True)
        return (v - m) / jnp.sqrt(s + eps)

    def _ln_t(v, eps=1e-05):
        m = jnp.mean(v, axis=-1, keepdims=True)
        s = jnp.var(v, axis=-1, keepdims=True)
        return (v - m) / jnp.sqrt(s + eps)

    def _to_tokens(v):
        B_, C_, H_, W_ = v.shape
        return v.reshape(B_, C_, H_ * W_).transpose(0, 2, 1)

    def _from_tokens(t, like):
        B_, C_, H_, W_ = like.shape
        return t.transpose(0, 2, 1).reshape(B_, C_, H_, W_)
    x = _L0_conv_ref(x, L0_conv_in_gamma, L0_conv_in_beta, L0_conv_wq, L0_conv_bq, L0_conv_wk, L0_conv_bk, L0_conv_wv, L0_conv_bv, L0_conv_wo, L0_conv_bo, L0_conv_w_cbr, L0_conv_b_cbr, L0_conv_g_cbr, L0_conv_be_cbr)
    t = _to_tokens(x)
    t = t + _L1_attn_ref(_ln_t(t))
    t = t + _L1_ffn_ref(_ln_t(t), L1_ffn_gate_w, L1_ffn_gate_b, L1_ffn_weight1, L1_ffn_weight2)
    x = _from_tokens(t, x)
    return x

_drawn_inputs = setup_inputs


def setup_inputs(seed=0):
    import zlib

    import numpy as np

    out = dict(_drawn_inputs(seed))
    spreads = {'L0_conv_in_gamma': (1.0, 0.6),
     'L0_conv_in_beta': (0.0, 0.1),
     'L0_conv_g_cbr': (1.0, 0.2),
     'L0_conv_be_cbr': (0.0, 0.1),
     'L1_ffn_gate_b': (0.0, 0.8)}
    factors = {'L0_conv_bq': 8.0,
     'L0_conv_bk': 64.0,
     'L0_conv_b_cbr': 64.0,
     'L1_ffn_gate_w': 64.0,
     'L1_ffn_weight1': 64.0,
     'L1_ffn_weight2': 64.0}
    for name, (base, spread) in spreads.items():
        noise = np.random.default_rng([zlib.crc32(name.encode()), seed]).standard_normal(out[name].shape)
        drawn = base * np.exp(spread * noise) if base else spread * noise
        out[name] = jnp.asarray(drawn.astype(out[name].dtype))
    for name, factor in factors.items():
        out[name] = (out[name] * factor).astype(out[name].dtype)
    return out
```

```python
from contextlib import ExitStack

import numpy as np

import concourse.bass as bass
from concourse import mybir

F32 = mybir.dt.float32
ALU = mybir.AluOpType
ACT = mybir.ActivationFunctionType
AX = mybir.AxisListType

B, C, N = 4, 32, 256
P = B * C
J = N // P
E, H, K = 16, 128, 8
EP = 32
GE = P // C
NG = E // GE
EPS = 1e-5
TAKEN = -3.0e38

VEC = ["in_gamma", "in_beta", "bq", "bk", "bv", "bo", "g_cbr", "be_cbr", "gate_b"]
MAT = ["wqT", "wkT", "wv", "woT", "wcT", "gateT"]
CON = ["ident", "center", "mean", "block", "zmask"]


def hybrid_block(nc, x, vecs, mats, cons, masks, w1, w2, rows, out):
    with ExitStack() as ctx:
        def sb(name, shape):
            return ctx.enter_context(nc.sbuf_tensor(name, shape, F32))

        names = """eps_set lnv lnu lny lnt x_in vecs_in wqk_in wvo_in ident_in cons_in masks_in w1_in w2_in rows_in out_done
            exp_table gelu_table ones_set hdiag_zero vaug_ones one_set neg_set
            stats agg rstd scale shift xn_ready
            prod1_mm prod1_ready prod2_mm prod2_ready bias1_ready xres_ready
            q_mm k_mm q_ready k_ready v_mm v_ready
            s_mm max_ready mxr_zero maxr_ready st_mm rt_mm r_ready shifted exp_ready pv_mm rsum_ready
            onu_ready ono_ready u_mm o_mm ustats uagg urstd uscale ushift uaff y_ready
            yc_mm ysq_ready yvar_ready yrstd_ready xt_ready g_mm g_ready xc_mm xc_ready
            tc_mm tsq_ready tcs_ready var_mm raw_mm trstd_ready lraw_ready logits_ready
            x2c_ready x2t_mm x2t_ready top_ready negmax_ready gexp_ready taken_ready
            wm_ready grec_ready gdiag_ready wt_mm wt_ready pool_mm pool_ready h_mm h_ready
            z_mm z_ready f_mm final_ready"""
        s = {n: ctx.enter_context(nc.semaphore(n)) for n in names.split()}

        ps = ctx.enter_context(nc.psum_tensor("ps", [P, 8, 512], F32))

        xs = sb("xs", [P, N])
        vec = sb("vec", [P, len(VEC)])
        mat = sb("mat", [P, len(MAT), P])
        con = sb("con", [P, len(CON), P])
        v = {n: vec[:, i:i + 1] for i, n in enumerate(VEC)}
        m = {n: mat[:, i, :] for i, n in enumerate(MAT)}
        c = {n: con[:, i, :] for i, n in enumerate(CON)}
        msk = sb("msk", [P, 2, E * B])
        w1s = sb("w1s", [P, NG, H])
        w2s = sb("w2s", [P, E, C])
        row = sb("row", [E, 4, P + C])
        ones = sb("ones", [1, N])
        neg = sb("neg", [P, P])
        eps = sb("eps", [P, 1])
        lnv, lnu, lny, lnt = sb("lnv", [P, 1]), sb("lnu", [P, 1]), sb("lny", [P, J, B]), sb("lnt", [P, N])

        bst, bag = sb("bst", [P, 6]), sb("bag", [P, 2])
        rstd, sca, shi = sb("rstd", [P, 1]), sb("sca", [P, 1]), sb("shi", [P, 1])
        xn = sb("xn", [P, N])
        prod1 = sb("prod1", [P, P])
        vmat = sb("vmat", [P, 2, P])
        bias1 = sb("bias1", [P, 1])
        xres = sb("xres", [P, N])
        q, k = sb("q", [P, N]), sb("k", [P, N])
        vaug = sb("vaug", [P, J, B, 2 * C + 1])
        mx = sb("mx", [P, J, B])
        mxr = sb("mxr", [P, 2, J, B, C])
        rr = sb("rr", [P, N])
        pt = sb("pt", [P, B, J, N])
        rs = sb("rs", [P, J, B])
        on = sb("on", [P, 2, J, P])
        ubst, ubag = sb("ubst", [P, 6]), sb("ubag", [P, 2])
        urstd, usca, ushi = sb("urstd", [P, 1]), sb("usca", [P, 1]), sb("ushi", [P, 1])
        uaff = sb("uaff", [P, N])
        y = sb("y", [P, N])
        ysq = sb("ysq", [P, J, B, C])
        yvar, yrstd = sb("yvar", [P, J, B]), sb("yrstd", [P, J, B])
        xt = sb("xt", [P, J, B, C])
        gbd = sb("gbd", [P, P])
        xc = sb("xc", [P, N])
        tsq, tcs = sb("tsq", [P, N]), sb("tcs", [P, N])
        trstd, lraw, logit = sb("trstd", [P, N]), sb("lraw", [P, N]), sb("logit", [P, N])
        x2c = sb("x2c", [P, N])
        x2t = sb("x2t", [P, J, B, GE, C])
        top, negmax, gsum, grec = sb("top", [P, K]), sb("negmax", [P, 1]), sb("gsum", [P, 1]), sb("grec", [P, 1])
        gexp, taken, wm = sb("gexp", [P, N]), sb("taken", [P, N]), sb("wm", [P, N])
        gdiag = sb("gdiag", [P, B * E])
        wt = sb("wt", [P, J, B, E])
        pooled = sb("pooled", [P, NG, GE, B])
        hdiag = sb("hdiag", [P, E, P])
        zbd = sb("zbd", [P, B, C])
        fin = sb("fin", [P, N])

        def bank(i, n=512, at=0):
            return ps[:, i, at:at + n]

        def img(t, b):
            return t[b * C:(b + 1) * C, :]

        def chunk(t, j):
            return t[:, j * P:(j + 1) * P]

        Q, KK = bank(4, N), bank(5, N)
        PROD1, PROD2, BIAS1 = bank(6, 2 * P), bank(7, P), bank(7, 1, 2 * P)
        V = bank(7).rearrange("p (i k b c) -> p i k b c", i=J, k=2, b=B)
        RT = [bank(0, N), bank(3, N)]
        O = ps[:, 1:3, 0:B * (2 * C + 1)].rearrange("p j (b c) -> p j b c", b=B)
        U, OO = bank(0, N), bank(3, N)
        YC = bank(4, N).rearrange("p (j b c) -> p j b c", j=J, b=B)
        G, XC, TC, T = bank(5, P), bank(6, N), bank(7, N), bank(1, N)
        VAR, RAW, X2T = bank(2, N), bank(4, N), bank(5, N)
        WT, POOL, HH, Z = bank(6, J * B * E), bank(0, B * E), bank(3, E * B), bank(7, C)

        block = ctx.enter_context(nc.Block())

        @block.sync
        def _(sp):
            sp.dma_start(xs[:, :], x).then_inc(s["x_in"], 16)
            sp.dma_start(mat[:, 0:2, :], mats[:, 0:2, :]).then_inc(s["wqk_in"], 16)
            sp.dma_start(con[:, 0:1, :], cons[:, 0:1, :]).then_inc(s["ident_in"], 16)
            sp.dma_start(con[:, 1:, :], cons[:, 1:, :]).then_inc(s["cons_in"], 16)
            sp.dma_start(w1s[:, :, :], w1).then_inc(s["w1_in"], 16)
            sp.dma_start(w2s[:, :, :], w2).then_inc(s["w2_in"], 16)
            sp.wait_ge(s["final_ready"], 1)
            sp.dma_start(out, fin[:, :]).then_inc(s["out_done"], 16)
            sp.wait_ge(s["out_done"], 16)

        @block.gpsimd
        def _(pool):
            nc.gpsimd.memset(eps[:, :], EPS).then_inc(s["eps_set"], 1)
            nc.gpsimd.memset(neg[:, :], -1.0 / C).then_inc(s["neg_set"], 1)
            nc.gpsimd.memset(ones[:, :], 1.0).then_inc(s["ones_set"], 1)
            nc.gpsimd.memset(mxr[:, :, :, :, :], 0.0).then_inc(s["mxr_zero"], 1)
            nc.gpsimd.memset(vaug[:, :, :, :], 1.0).then_inc(s["vaug_ones"], 1)
            nc.gpsimd.memset(hdiag[:, :, :], 0.0).then_inc(s["hdiag_zero"], 1)
            pool.wait_ge(s["trstd_ready"], 1)
            pool.wait_ge(s["tcs_ready"], 1)
            nc.gpsimd.tensor_tensor(x2c[:, :], tcs[:, :], trstd[:, :], ALU.mult).then_inc(s["x2c_ready"], 1)

        @block.scalar
        def _(act):
            act.dma_start(vec[:, :], vecs).then_inc(s["vecs_in"], 16)
            act.dma_start(mat[:, 2:, :], mats[:, 2:, :]).then_inc(s["wvo_in"], 16)
            act.dma_start(msk[:, :, :], masks).then_inc(s["masks_in"], 16)
            act.dma_start(row[:, :, :], rows).then_inc(s["rows_in"], 16)
            nc.scalar.preload_act_table_set("natural_log_exp_and_others")

            def rsqrt(dst, var, log, logged, done):
                nc.scalar.activation(log, var, ACT.Ln, bias=eps[:, :]).then_inc(logged, 1)
                act.wait_ge(logged, 1)
                nc.scalar.activation(dst, log, ACT.Exp, scale=-0.5).then_inc(done, 1)

            act.wait_ge(s["eps_set"], 1)
            act.wait_ge(s["agg"], 1)
            rsqrt(rstd[:, :], bag[:, 1:2], lnv[:, :], s["lnv"], s["rstd"])

            act.wait_ge(s["prod1_mm"], 1)
            nc.scalar.copy(prod1[:, :], PROD1[:, 0:P]).then_inc(s["prod1_ready"], 1)
            nc.scalar.copy(vmat[:, 0, :], PROD1[:, P:2 * P]).then_inc(s["prod1_ready"], 1)
            act.wait_ge(s["prod2_mm"], 1)
            act.wait_ge(s["vecs_in"], 16)
            nc.scalar.copy(vmat[:, 1, :], PROD2).then_inc(s["prod2_ready"], 1)
            nc.scalar.activation(bias1[:, :], BIAS1, ACT.Identity, bias=v["bo"]).then_inc(s["bias1_ready"], 1)
            act.wait_ge(s["bias1_ready"], 1)
            act.wait_ge(s["x_in"], 16)
            nc.scalar.activation(xres[:, :], xs[:, :], ACT.Identity, bias=bias1[:, :]).then_inc(s["xres_ready"], 1)
            act.wait_ge(s["k_mm"], 1)
            nc.scalar.activation(k[:, :], KK, ACT.Identity, bias=v["bk"]).then_inc(s["k_ready"], 1)
            act.wait_ge(s["vaug_ones"], 1)
            act.wait_ge(s["v_mm"], 1)
            for i in range(J):
                nc.scalar.copy(vaug[:, i, :, 0:2 * C].rearrange("p b (k c) -> p k b c", k=2),
                               V[:, i, :, :, :]).then_inc(s["v_ready"], 1)
            act.wait_ge(s["rt_mm"], 1)
            nc.scalar.copy(rr[0:2 * C, :], RT[0][0:2 * C, :]).then_inc(s["r_ready"], 1)
            for b in range(B):
                act.wait_ge(s["shifted"], b + 1)
                nc.scalar.activation(pt[:, b, :, :].rearrange("p i n -> p (i n)"), bank(4 + b), ACT.Exp,
                                     scale=float(C) ** -0.5).then_inc(s["exp_ready"], 1)
            act.wait_ge(s["uagg"], 1)
            rsqrt(urstd[:, :], ubag[:, 1:2], lnu[:, :], s["lnu"], s["urstd"])
            act.wait_ge(s["yc_mm"], 1)
            nc.scalar.activation(ysq[:, :, :, :], YC, ACT.Square, scale=float(C) ** -0.5).then_inc(s["ysq_ready"], 1)
            act.wait_ge(s["yvar_ready"], 1)
            rsqrt(yrstd[:, :, :], yvar[:, :, :], lny[:, :, :], s["lny"], s["yrstd_ready"])
            act.wait_ge(s["xc_mm"], 1)
            nc.scalar.copy(xc[:, :], XC).then_inc(s["xc_ready"], 1)
            act.wait_ge(s["tc_mm"], 1)
            nc.scalar.activation(tsq[:, :], TC, ACT.Square).then_inc(s["tsq_ready"], 1)
            act.wait_ge(s["var_mm"], 1)
            rsqrt(trstd[:, :], VAR, lnt[:, :], s["lnt"], s["trstd_ready"])
            act.wait_ge(s["logits_ready"], 1)
            act.wait_ge(s["negmax_ready"], 1)
            nc.scalar.activation(gexp[:, :], logit[:, :], ACT.Exp, bias=negmax[:, :],
                                 accum_out=gsum[:, :]).then_inc(s["gexp_ready"], 1)
            act.wait_ge(s["x2t_mm"], 1)
            for j in range(J):
                nc.scalar.copy(x2t[:, j, :, :, :], chunk(X2T, j).rearrange("p (b c) -> p b c", b=B).unsqueeze(2)
                               .to_broadcast([P, B, GE, C])).then_inc(s["x2t_ready"], 1)
            nc.scalar.preload_act_table(ACT.Gelu)
            act.wait_ge(s["h_mm"], 1)
            act.wait_ge(s["hdiag_zero"], 1)
            hd = hdiag[:, :, :]
            diag = bass.AP(hd.tensor, hd.offset, [list(hd.ap[0]), [P + 1, E], [EP, B]])
            nc.scalar.activation(diag, HH.rearrange("p (e b) -> p e b", e=E), ACT.Gelu).then_inc(s["h_ready"], 1)

        @block.vector
        def _(dve):
            dve.wait_ge(s["x_in"], 16)
            nc.vector.bn_stats(bst[:, :], xs[:, :]).then_inc(s["stats"], 1)
            dve.wait_ge(s["stats"], 1)
            nc.vector.bn_aggr(bag[:, :], bst[:, :]).then_inc(s["agg"], 1)
            dve.wait_ge(s["rstd"], 1)
            dve.wait_ge(s["vecs_in"], 16)
            nc.vector.tensor_tensor(sca[:, :], rstd[:, :], v["in_gamma"], ALU.mult).then_inc(s["scale"], 1)
            dve.wait_ge(s["scale"], 1)
            nc.vector.scalar_tensor_tensor(shi[:, :], bag[:, 0:1], sca[:, :], v["in_beta"],
                                           ALU.mult, ALU.subtract).then_inc(s["shift"], 1)
            dve.wait_ge(s["shift"], 1)
            nc.vector.tensor_scalar(xn[:, :], xs[:, :], sca[:, :], shi[:, :],
                                    ALU.mult, ALU.subtract).then_inc(s["xn_ready"], 1)
            dve.wait_ge(s["q_mm"], 1)
            nc.vector.tensor_scalar(q[:, :], Q, v["bq"], None, ALU.add).then_inc(s["q_ready"], 1)
            for b in range(B):
                dve.wait_ge(s["s_mm"], b + 1)
                nc.vector.tensor_reduce(mx[:, :, b], bank(b).rearrange("p (j m) -> p j m", j=J),
                                        AX.X, ALU.max).then_inc(s["max_ready"], 1)
                if b % 2:
                    two = slice(b - 1, b + 1)
                    dve.wait_ge(s["mxr_zero"], 1)
                    dve.wait_ge(s["max_ready"], b + 1)
                    nc.vector.tensor_copy(mxr[:, b // 2, :, two, :], mx[:, :, two].unsqueeze(3)
                                          .to_broadcast([P, J, 2, C])).then_inc(s["maxr_ready"], 1)
            dve.wait_ge(s["rt_mm"], 2)
            nc.vector.tensor_copy(rr[2 * C:4 * C, :], RT[1][2 * C:4 * C, :]).then_inc(s["r_ready"], 1)
            dve.wait_ge(s["pv_mm"], B)
            nc.vector.reciprocal(rs[:, :, :], O[:, :, :, 2 * C]).then_inc(s["rsum_ready"], 1)
            dve.wait_ge(s["rsum_ready"], 1)
            rsb = rs[:, :, :].unsqueeze(3).to_broadcast([P, J, B, C])
            for kind, done in ((1, s["onu_ready"]), (0, s["ono_ready"])):
                nc.vector.tensor_tensor(on[:, kind, :, :].rearrange("p j (b c) -> p j b c", b=B),
                                        O[:, :, :, kind * C:(kind + 1) * C], rsb, ALU.mult).then_inc(done, 1)
            dve.wait_ge(s["u_mm"], 1)
            nc.vector.bn_stats(ubst[:, :], U).then_inc(s["ustats"], 1)
            dve.wait_ge(s["ustats"], 1)
            nc.vector.bn_aggr(ubag[:, :], ubst[:, :]).then_inc(s["uagg"], 1)
            dve.wait_ge(s["urstd"], 1)
            nc.vector.tensor_tensor(usca[:, :], urstd[:, :], v["g_cbr"], ALU.mult).then_inc(s["uscale"], 1)
            dve.wait_ge(s["uscale"], 1)
            nc.vector.scalar_tensor_tensor(ushi[:, :], ubag[:, 0:1], usca[:, :], v["be_cbr"],
                                           ALU.mult, ALU.subtract).then_inc(s["ushift"], 1)
            dve.wait_ge(s["ushift"], 1)
            nc.vector.tensor_scalar(uaff[:, :], U, usca[:, :], ushi[:, :],
                                    ALU.mult, ALU.subtract).then_inc(s["uaff"], 1)
            dve.wait_ge(s["uaff"], 1)
            dve.wait_ge(s["o_mm"], 1)
            nc.vector.scalar_tensor_tensor(y[:, :], uaff[:, :], 0.0, OO, ALU.max, ALU.add).then_inc(s["y_ready"], 1)
            dve.wait_ge(s["ysq_ready"], 1)
            nc.vector.tensor_reduce(yvar[:, :, :], ysq[:, :, :, :], AX.X, ALU.add).then_inc(s["yvar_ready"], 1)
            dve.wait_ge(s["yrstd_ready"], 1)
            nc.vector.tensor_tensor(xt[:, :, :, :], YC, yrstd[:, :, :].unsqueeze(3).to_broadcast([P, J, B, C]),
                                    ALU.mult).then_inc(s["xt_ready"], 1)
            dve.wait_ge(s["g_mm"], 1)
            dve.wait_ge(s["cons_in"], 16)
            nc.vector.tensor_tensor(gbd[:, :], G, c["block"], ALU.mult).then_inc(s["g_ready"], 1)
            dve.wait_ge(s["tsq_ready"], 1)
            nc.vector.tensor_copy(tcs[:, :], TC).then_inc(s["tcs_ready"], 1)
            dve.wait_ge(s["trstd_ready"], 1)
            dve.wait_ge(s["raw_mm"], 1)
            nc.vector.tensor_tensor(lraw[:, :], RAW, trstd[:, :], ALU.mult).then_inc(s["lraw_ready"], 1)
            dve.wait_ge(s["lraw_ready"], 1)
            nc.vector.tensor_scalar(logit[:, :], lraw[:, :], v["gate_b"], None, ALU.add).then_inc(s["logits_ready"], 1)
            dve.wait_ge(s["logits_ready"], 1)
            nc.vector.max(top[:, :], logit[:, :]).then_inc(s["top_ready"], 1)
            dve.wait_ge(s["top_ready"], 1)
            nc.vector.tensor_scalar(negmax[:, :], top[:, 0:1], -1.0, None, ALU.mult).then_inc(s["negmax_ready"], 1)
            nc.vector.match_replace(taken[:, :], top[:, :], logit[:, :], TAKEN).then_inc(s["taken_ready"], 1)
            dve.wait_ge(s["taken_ready"], 1)
            dve.wait_ge(s["gexp_ready"], 1)
            nc.vector.scalar_tensor_tensor(wm[:, :], taken[:, :], TAKEN, gexp[:, :],
                                           ALU.is_equal, ALU.mult).then_inc(s["wm_ready"], 1)
            nc.vector.reciprocal(grec[:, :], gsum[:, :]).then_inc(s["grec_ready"], 1)
            dve.wait_ge(s["grec_ready"], 1)
            dve.wait_ge(s["masks_in"], 16)
            nc.vector.tensor_scalar(gdiag[:, :], msk[:, 1, :], grec[:, :], None, ALU.mult).then_inc(s["gdiag_ready"], 1)
            dve.wait_ge(s["wt_mm"], 1)
            nc.vector.tensor_copy(wt[:, :, :, :].rearrange("p j b e -> p (j b e)"), WT).then_inc(s["wt_ready"], 1)
            dve.wait_ge(s["pool_mm"], 1)
            nc.vector.tensor_tensor(pooled[:, :, :, :],
                                    POOL.rearrange("p (b g e) -> p g e b", b=B, g=NG),
                                    msk[:, 0, :].rearrange("p (g e b) -> p g e b", g=NG, e=GE),
                                    ALU.mult).then_inc(s["pool_ready"], 1)
            dve.wait_ge(s["z_mm"], 1)
            nc.vector.scalar_tensor_tensor(zbd[:, :, :], Z.unsqueeze(1).to_broadcast([P, B, C]), grec[:, :],
                                           c["zmask"].rearrange("p (b c) -> p b c", b=B),
                                           ALU.mult, ALU.mult).then_inc(s["z_ready"], 1)
            dve.wait_ge(s["f_mm"], 1)
            nc.vector.tensor_copy(fin[:, :], T).then_inc(s["final_ready"], 1)

        @block.tensor
        def _(pe):
            mm = nc.tensor.matmul
            pe.wait_ge(s["wvo_in"], 16)
            mm(PROD1[:, 0:P], m["woT"], m["wv"], start=True, stop=True)
            mm(PROD1[:, P:2 * P], m["wv"], m["woT"], start=True, stop=True).then_inc(s["prod1_mm"], 1)
            pe.wait_ge(s["prod1_ready"], 1)
            pe.wait_ge(s["vecs_in"], 16)
            mm(PROD2, prod1[:, :], m["wcT"], start=True, stop=True)
            mm(BIAS1, m["woT"], v["bv"], start=True, stop=True).then_inc(s["prod2_mm"], 1)
            pe.wait_ge(s["xn_ready"], 1)
            pe.wait_ge(s["wqk_in"], 16)
            mm(Q, m["wqT"], xn[:, :], start=True, stop=True).then_inc(s["q_mm"], 1)
            mm(KK, m["wkT"], xn[:, :], start=True, stop=True).then_inc(s["k_mm"], 1)
            pe.wait_ge(s["prod1_ready"], 2)
            pe.wait_ge(s["prod2_ready"], 1)
            pe.wait_ge(s["bias1_ready"], 1)
            for i in range(J):
                last = mm(V[:, i, :, :, :].rearrange("p k b c -> p (k b c)"), chunk(xn, i),
                          vmat[:, :, :].rearrange("p k c -> p (k c)"), start=True, stop=True)
            last.then_inc(s["v_mm"], 1)
            pe.wait_ge(s["q_ready"], 1)
            pe.wait_ge(s["k_ready"], 1)
            for j in range(J):
                for b in range(B):
                    last = mm(bank(b, N, j * N), chunk(img(q, b), j), img(k, b), start=True, stop=True)
                    if j == J - 1:
                        last.then_inc(s["s_mm"], 1)
            pe.wait_ge(s["v_ready"], J)
            for i in range(J):
                for b in range(B):
                    mm(bank(4 + b, N, i * N), chunk(img(k, b), i), img(q, b),
                       start=(i == 0), stop=False, skip_group_check=True)
            pe.wait_ge(s["ident_in"], 16)
            pe.wait_ge(s["neg_set"], 1)
            for p in range(2):
                pe.wait_ge(s["maxr_ready"], p + 1)
                for j in range(J):
                    last = nc.tensor.transpose(chunk(RT[p], j), mxr[:, p, j, :, :].rearrange("p b c -> p (b c)"),
                                               c["ident"])
                last.then_inc(s["rt_mm"], 1)
                pe.wait_ge(s["r_ready"], p + 1)
                for b in (2 * p, 2 * p + 1):
                    for i in range(J):
                        last = mm(bank(4 + b, N, i * N), img(neg, b), img(rr, b),
                                  start=False, stop=True, skip_group_check=True)
                    last.then_inc(s["shifted"], 1)
            pe.wait_ge(s["xres_ready"], 1)
            pe.wait_ge(s["rows_in"], 16)
            pe.wait_ge(s["ones_set"], 1)
            mm(U, m["wcT"], xres[:, :], start=True, stop=False, skip_group_check=True)
            mm(U, row[0:1, 1, 0:P], ones[:, :], start=False, stop=False, skip_group_check=True)
            mm(OO, c["ident"], xres[:, :], start=True, stop=False, skip_group_check=True)
            for b in range(B):
                pe.wait_ge(s["exp_ready"], b + 1)
                for j in range(J):
                    for i in range(J):
                        last = mm(O[:, j, b, :], pt[:, b, i, j * P:(j + 1) * P], vaug[:, i, b, :],
                                  start=(i == 0), stop=(i == J - 1))
                last.then_inc(s["pv_mm"], 1)
            for kind, acc, ready, done in ((1, U, s["onu_ready"], s["u_mm"]), (0, OO, s["ono_ready"], s["o_mm"])):
                pe.wait_ge(ready, 1)
                for j in range(J):
                    last = mm(chunk(acc, j), on[:, kind, j, :], c["ident"],
                              start=False, stop=True, skip_group_check=True)
                last.then_inc(done, 1)
            pe.wait_ge(s["y_ready"], 1)
            pe.wait_ge(s["cons_in"], 16)
            for j in range(J):
                last = mm(YC[:, j, :, :].rearrange("p b c -> p (b c)"), chunk(y, j), c["center"],
                          start=True, stop=True)
            last.then_inc(s["yc_mm"], 1)
            mm(TC, c["center"], y[:, :], start=True, stop=False, skip_group_check=True)
            mm(T, c["ident"], y[:, :], start=True, stop=False, skip_group_check=True)
            pe.wait_ge(s["xt_ready"], 1)
            xtj = [xt[:, j, :, :].rearrange("p b c -> p (b c)") for j in range(J)]
            for j in range(J):
                last = mm(G, xtj[j], xtj[j], start=(j == 0), stop=(j == J - 1))
            last.then_inc(s["g_mm"], 1)
            for j in range(J):
                last = nc.tensor.transpose(chunk(XC, j), xtj[j], c["ident"])
            last.then_inc(s["xc_mm"], 1)
            pe.wait_ge(s["g_ready"], 1)
            pe.wait_ge(s["xc_ready"], 1)
            mm(TC, gbd[:, :], xc[:, :], start=False, stop=True, skip_group_check=True).then_inc(s["tc_mm"], 1)
            mm(T, gbd[:, :], xc[:, :], start=False, stop=False, skip_group_check=True)
            pe.wait_ge(s["tsq_ready"], 1)
            mm(VAR, c["mean"], tsq[:, :], start=True, stop=True).then_inc(s["var_mm"], 1)
            pe.wait_ge(s["tcs_ready"], 1)
            mm(RAW, m["gateT"], tcs[:, :], start=True, stop=True).then_inc(s["raw_mm"], 1)
            mm(HH, row[:, 0, 0:H], row[:, 2, 0:E * B], start=True, stop=False, skip_group_check=True)
            mm(Z, row[:, 3, 0:P], row[:, 1, P:P + C], start=True, stop=False,
               skip_group_check=True)
            pe.wait_ge(s["x2c_ready"], 1)
            for j in range(J):
                last = nc.tensor.transpose(chunk(X2T, j), chunk(x2c, j), c["ident"])
            last.then_inc(s["x2t_mm"], 1)
            pe.wait_ge(s["wm_ready"], 1)
            pe.wait_ge(s["gdiag_ready"], 1)
            for j in range(J):
                last = mm(WT[:, j * B * E:(j + 1) * B * E], chunk(wm, j), gdiag[:, :], start=True, stop=True)
            last.then_inc(s["wt_mm"], 1)
            pe.wait_ge(s["wt_ready"], 1)
            pe.wait_ge(s["x2t_ready"], J)
            for b in range(B):
                for j in range(J):
                    last = mm(POOL[:, b * E:(b + 1) * E], x2t[:, j, b, :, :].rearrange("p g c -> p (g c)"),
                              wt[:, j, b, :],
                              start=(j == 0), stop=(j == J - 1))
            last.then_inc(s["pool_mm"], 1)
            pe.wait_ge(s["pool_ready"], 1)
            pe.wait_ge(s["w1_in"], 16)
            for g in range(NG):
                last = mm(HH[:, g * GE * B:(g + 1) * GE * B], w1s[:, g, :],
                          pooled[:, g, :, :].rearrange("p e b -> p (e b)"),
                          start=False, stop=True, skip_group_check=True)
            last.then_inc(s["h_mm"], 1)
            pe.wait_ge(s["h_ready"], 1)
            pe.wait_ge(s["w2_in"], 16)
            for e in range(E):
                last = mm(Z, hdiag[:, e, :], w2s[:, e, :], start=False, stop=(e == E - 1), skip_group_check=True)
            last.then_inc(s["z_mm"], 1)
            pe.wait_ge(s["z_ready"], 1)
            mm(T, zbd[:, :, :].rearrange("p b c -> p (b c)"), wm[:, :],
               start=False, stop=True, skip_group_check=True).then_inc(s["f_mm"], 1)


def kernel(**inputs):
    import concourse.bacc as bacc
    from concourse.bass_utils import run_bass_kernel_spmd

    a = {n: np.asarray(t) for n, t in inputs.items()}
    f = np.float32

    def tiled(t):
        return np.tile(t, B)

    def diagonal(t):
        d = np.zeros((B, C, B, t.shape[1]), f)
        for b in range(B):
            d[b, :, b, :] = t
        return d.reshape(P, -1)

    L = "L0_conv_"
    gate_b = np.zeros(EP, f)
    gate_b[:E] = a["L1_ffn_gate_b"]
    cols = [a[L + n] for n in VEC[:-1]] + [gate_b]
    vecs = np.ascontiguousarray(np.stack([tiled(t) for t in cols], axis=1))

    gateT = np.zeros((C, EP), f)
    gateT[:, :E] = a["L1_ffn_gate_w"].T
    mats = np.stack([diagonal(t) for t in (a[L + "wq"].T, a[L + "wk"].T, a[L + "wv"], a[L + "wo"].T,
                                           a[L + "w_cbr"].T, gateT)], axis=1)

    blk = diagonal(np.ones((C, C), f))
    zmask = diagonal(np.concatenate([np.ones((E, C), f), np.zeros((EP - E, C), f)]))
    cons = np.stack([np.eye(P, dtype=f), np.eye(P, dtype=f) - blk / f(C), blk / f(C), blk, zmask], axis=1)
    masks = np.zeros((P, 2, E * B), f)
    masks[:, 0, :] = np.broadcast_to(np.eye(GE, dtype=f)[:, None, None, :, None],
                                     (GE, C, NG, GE, B)).reshape(P, E * B)
    masks[:, 1, :].reshape(P, B, E)[:] = np.eye(P, dtype=f).reshape(P, B, EP)[:, :, :E]

    w1, w2 = a["L1_ffn_weight1"], a["L1_ffn_weight2"]
    w1g = np.ascontiguousarray(w1[:, :C, :].reshape(NG, GE, C, H).transpose(1, 2, 0, 3).reshape(P, NG, H))
    w2g = np.ascontiguousarray(w2[:, :H, :].transpose(1, 0, 2))
    rows = np.zeros((E, 4, P + C), f)
    rows[:, 0, :H] = w1[:, C, :]
    rows[0, 1, :P] = tiled(a[L + "b_cbr"])
    rows[:, 1, P:] = w2[:, H, :]
    rows[:, 2, :E * B] = np.repeat(np.eye(E, dtype=f), B, axis=1)
    rows[:, 3, :P].reshape(E, B, EP)[:, :, :E] = np.eye(E, dtype=f)[:, None, :]

    arrays = {"x": np.ascontiguousarray(a["x"].reshape(P, N)), "vecs": vecs, "mats": mats, "cons": cons,
              "masks": masks, "w1": w1g, "w2": w2g, "rows": rows}
    nc = bacc.Bacc("TRN2", target_bir_lowering=False, num_devices=1)
    args = [nc.dram_tensor(n, t.shape, F32, kind="ExternalInput").ap() for n, t in arrays.items()]
    args.append(nc.dram_tensor("out", (P, N), F32, kind="ExternalOutput").ap())
    hybrid_block(nc, *args)
    r = run_bass_kernel_spmd(nc, [arrays], core_ids=[0])
    return r.results[0]["out"].reshape(B, C, 16, 16)
```

```python
from contextlib import ExitStack

import numpy as np

import concourse.bass as bass
from concourse import mybir

F32 = mybir.dt.float32
ALU = mybir.AluOpType
ACT = mybir.ActivationFunctionType
AX = mybir.AxisListType

B, C, N = 4, 32, 256
P = B * C
J = N // P
E, H, K = 16, 128, 8
EP = 32
GE = P // C
NG = E // GE
EPS = 1e-5
TAKEN = -3.0e38
WARM = [30, 2, 8, 6, 2, 2, 6, 12, 2, 1, 4, 4]

VEC = ["in_gamma", "in_beta", "bq", "bk", "bv", "bo", "g_cbr", "be_cbr", "gate_b"]
MAT = ["wv", "woT", "wcT", "gateT"]
CON = ["ident", "center", "mean", "block"]


def hybrid_block(nc, x, wqkv, mats, cons, masks, w1, w2, rows, out):
    with ExitStack() as ctx:
        def sb(name, shape):
            return ctx.enter_context(nc.sbuf_tensor(name, shape, F32))

        names = """x_in wqkv_in wvo_in ident_in cons_in masks_in w1_in w2_in rows_in out_done
            eps_set ones_set hdiag_zero qm_zero warm_set
            stats agg lnv rstd scale shift xn_ready
            prod1_mm prod1_ready prod2_mm prod2_ready bias1_ready xres_ready
            q_mm k_mm q_dve q_act k_ready v_mm v_ready
            s_mm max_ready exp_ready pt_mm pt_dve pt_act pv_mm rsum_ready
            onu_ready ono_ready u_mm o_mm ustats uagg lnu urstd uscale ushift uaff y_ready
            yc_mm ysq_ready yvar_ready lny yrstd_ready xt_ready g_mm g_ready xc_mm xc_ready
            tc_mm tsq_ready tcs_ready var_mm raw_mm lnt trstd_ready logits_ready
            x2c_ready x2t_mm x2t_ready top_ready negmax_ready gexp_ready taken_ready
            wm_ready grec_ready wt_mm wt_ready pool_mm rep_ready rept_mm pool_ready h_mm h_ready
            z_mm zsel_ready zsum_ready z_ready f_mm final_dve final_act"""
        s = {n: ctx.enter_context(nc.semaphore(n)) for n in names.split()}

        ps = ctx.enter_context(nc.psum_tensor("ps", [P, 8, 512], F32))

        xs = sb("xs", [P, N])
        qkv = sb("qkv", [P, 2 * P + len(VEC)])
        mat = sb("mat", [P, len(MAT), P])
        con = sb("con", [P, len(CON), P])
        v = {n: qkv[:, 2 * P + i:2 * P + i + 1] for i, n in enumerate(VEC)}
        m = {n: mat[:, i, :] for i, n in enumerate(MAT)}
        wqT, wkT = qkv[:, 0:P], qkv[:, P:2 * P]
        c = {n: con[:, i, :] for i, n in enumerate(CON)}
        msk = sb("msk", [P, E * B + GE])
        w1s = sb("w1s", [P, NG, H])
        w2s = sb("w2s", [P, E, C])
        row = sb("row", [E, 4, P + C])
        ones = sb("ones", [1, N])
        warm = ctx.enter_context(nc.sbuf_tensor("warm", [P, 2 * P], mybir.dt.bfloat16))
        eps = sb("eps", [P, 1])
        lnv, lnu, lny, lnt = sb("lnv", [P, 1]), sb("lnu", [P, 1]), sb("lny", [P, J, B]), sb("lnt", [P, N])

        bst, bag = sb("bst", [P, 6]), sb("bag", [P, 2])
        rstd, sca, shi = sb("rstd", [P, 1]), sb("sca", [P, 1]), sb("shi", [P, 1])
        xn = sb("xn", [P, N])
        prod1 = sb("prod1", [P, P])
        vmat = sb("vmat", [P, 2, P])
        bias1 = sb("bias1", [P, 1])
        xres = sb("xres", [P, N])
        qm = sb("qm", [P, B, N])
        k = sb("k", [P, N])
        vt = sb("vt", [P, J, B, 2 * C])
        nmx, rsum = sb("nmx", [P, B, J]), sb("rsum", [P, J, B])
        prob = sb("prob", [P, B, J, N])
        pt = sb("pt", [P, B, J, N])
        rs = sb("rs", [P, J, B])
        on = sb("on", [P, 2, J, P])
        ubst, ubag = sb("ubst", [P, 6]), sb("ubag", [P, 2])
        urstd, usca, ushi = sb("urstd", [P, 1]), sb("usca", [P, 1]), sb("ushi", [P, 1])
        uaff = sb("uaff", [P, N])
        y = sb("y", [P, N])
        ysq = sb("ysq", [P, J, B, C])
        yvar, yrstd = sb("yvar", [P, J, B]), sb("yrstd", [P, J, B])
        xt = sb("xt", [P, J, B, C])
        gbd = sb("gbd", [P, P])
        xc = sb("xc", [P, N])
        tsq, tcs = sb("tsq", [P, N]), sb("tcs", [P, N])
        trstd, logit = sb("trstd", [P, N]), sb("logit", [P, N])
        x2c = sb("x2c", [P, N])
        x2t = sb("x2t", [P, J, B, C])
        top, negmax, gsum, grec = sb("top", [P, K]), sb("negmax", [P, 1]), sb("gsum", [P, 1]), sb("grec", [P, 1])
        gexp, taken, wm = sb("gexp", [P, N]), sb("taken", [P, N]), sb("wm", [P, N])
        wt = sb("wt", [P, J, B, EP])
        rep = sb("rep", [P, GE, C])
        pooled = sb("pooled", [P, NG, GE, B])
        hdiag = sb("hdiag", [P, NG, P])
        zsel, zsum = sb("zsel", [P, GE, C]), sb("zsum", [P, C])
        zbd = sb("zbd", [P, B, C])
        fin = sb("fin", [P, N])

        def bank(i, n=512, at=0):
            return ps[:, i, at:at + n]

        def img(t, b):
            return t[b * C:(b + 1) * C, :]

        def chunk(t, j):
            return t[:, j * P:(j + 1) * P]

        Q, KK = bank(4, N), bank(5, N)
        PROD1, PROD2, BIAS1 = bank(6, 2 * P), bank(3, P), bank(3, 1, 2 * P)
        V = bank(7).rearrange("p (i k b c) -> p i k b c", i=J, k=2, b=B)
        O = bank(0).rearrange("p (j b c) -> p j b c", j=J, b=B)
        U, OO = bank(1, N), bank(2, N)
        YC = bank(4, N).rearrange("p (j b c) -> p j b c", j=J, b=B)
        G, XC, TC = bank(5, P), bank(6, N), bank(7, N)
        T = [bank(1, P), bank(2, P)]
        VAR, RAW, X2T = bank(5, N), bank(4, N), bank(6, N)
        WT, POOL, REPT, HH, Z = bank(5, J * P), bank(4, C), bank(6, P), bank(0, E * B), bank(7, GE * C)
        IDLE = bank(3, 2 * P)

        block = ctx.enter_context(nc.Block())

        @block.sync
        def _(sp):
            sp.dma_start(xs[:, :], x).then_inc(s["x_in"], 16)
            sp.dma_start(qkv[:, :], wqkv).then_inc(s["wqkv_in"], 16)
            sp.dma_start(mat[:, :, :], mats).then_inc(s["wvo_in"], 16)
            sp.dma_start(con[:, :, :], cons).then_inc(s["cons_in"], 16)
            sp.dma_start(row[:, :, :], rows).then_inc(s["rows_in"], 16)
            sp.dma_start(msk[:, :], masks).then_inc(s["masks_in"], 16)
            sp.dma_start(w1s[:, :, :], w1).then_inc(s["w1_in"], 16)
            sp.dma_start(w2s[:, :, :], w2).then_inc(s["w2_in"], 16)
            sp.wait_ge(s["final_dve"], 1)
            sp.dma_start(out[:, 0:P], fin[:, 0:P]).then_inc(s["out_done"], 16)
            sp.wait_ge(s["out_done"], 32)

        @block.gpsimd
        def _(pool):
            nc.gpsimd.memset(warm[:, :], 0.0).then_inc(s["warm_set"], 1)
            nc.gpsimd.memset(eps[:, :], EPS).then_inc(s["eps_set"], 1)
            nc.gpsimd.memset(qm[:, :, :], 0.0).then_inc(s["qm_zero"], 1)
            nc.gpsimd.memset(ones[:, :], 1.0).then_inc(s["ones_set"], 1)
            nc.gpsimd.memset(hdiag[:, :, :], 0.0).then_inc(s["hdiag_zero"], 1)
            pool.wait_ge(s["trstd_ready"], 1)
            pool.wait_ge(s["tcs_ready"], 1)
            nc.gpsimd.tensor_tensor(x2c[:, :], tcs[:, :], trstd[:, :], ALU.mult).then_inc(s["x2c_ready"], 1)

        @block.scalar
        def _(act):
            nc.scalar.preload_act_table_set("natural_log_exp_and_others")

            def rsqrt(dst, var, log, logged, done):
                nc.scalar.activation(log, var, ACT.Ln, bias=eps[:, :]).then_inc(logged, 1)
                act.wait_ge(logged, 1)
                nc.scalar.activation(dst, log, ACT.Exp, scale=-0.5).then_inc(done, 1)

            act.wait_ge(s["eps_set"], 1)
            act.wait_ge(s["agg"], 1)
            rsqrt(rstd[:, :], bag[:, 1:2], lnv[:, :], s["lnv"], s["rstd"])
            act.wait_ge(s["prod1_mm"], 1)
            nc.scalar.copy(prod1[:, :], PROD1[:, 0:P]).then_inc(s["prod1_ready"], 1)
            nc.scalar.copy(vmat[:, 0, :], PROD1[:, P:2 * P]).then_inc(s["prod1_ready"], 1)
            act.wait_ge(s["k_mm"], 1)
            nc.scalar.activation(k[:, :], KK, ACT.Identity, bias=v["bk"]).then_inc(s["k_ready"], 1)
            act.wait_ge(s["prod2_mm"], 1)
            nc.scalar.copy(vmat[:, 1, :], PROD2).then_inc(s["prod2_ready"], 1)
            nc.scalar.activation(bias1[:, :], BIAS1, ACT.Identity, bias=v["bo"]).then_inc(s["bias1_ready"], 1)
            act.wait_ge(s["v_mm"], 1)
            for i in range(J):
                nc.scalar.copy(vt[:, i, :, :].rearrange("p b (k c) -> p k b c", k=2),
                               V[:, i, :, :, :]).then_inc(s["v_ready"], 1)
            for b in range(B):
                act.wait_ge(s["max_ready"], b + 1)
                for j in range(J):
                    nc.scalar.activation(prob[:, b, j, :], bank(b, N, j * N), ACT.Exp, bias=nmx[:, b, j:j + 1],
                                         accum_out=rsum[:, j, b:b + 1]).then_inc(s["exp_ready"], 1)
                if b == 0:
                    act.wait_ge(s["bias1_ready"], 1)
                    nc.scalar.activation(xres[:, :], xs[:, :], ACT.Identity,
                                         bias=bias1[:, :]).then_inc(s["xres_ready"], 1)
            act.wait_ge(s["pt_mm"], B)
            nc.scalar.copy(pt[:, B - 1, :, :].rearrange("p i n -> p (i n)"), bank(4 + B - 1)).then_inc(s["pt_act"], 1)
            act.wait_ge(s["uagg"], 1)
            rsqrt(urstd[:, :], ubag[:, 1:2], lnu[:, :], s["lnu"], s["urstd"])
            act.wait_ge(s["yc_mm"], 1)
            nc.scalar.activation(ysq[:, :, :, :], YC, ACT.Square, scale=float(C) ** -0.5)\
                .then_inc(s["ysq_ready"], 1)
            act.wait_ge(s["yvar_ready"], 1)
            rsqrt(yrstd[:, :, :], yvar[:, :, :], lny[:, :, :], s["lny"], s["yrstd_ready"])
            act.wait_ge(s["xc_mm"], 1)
            nc.scalar.copy(xc[:, :], XC).then_inc(s["xc_ready"], 1)
            act.wait_ge(s["tc_mm"], 1)
            nc.scalar.activation(tsq[:, :], TC, ACT.Square).then_inc(s["tsq_ready"], 1)
            act.wait_ge(s["var_mm"], 1)
            rsqrt(trstd[:, :], VAR, lnt[:, :], s["lnt"], s["trstd_ready"])
            act.wait_ge(s["x2t_mm"], 1)
            nc.scalar.copy(x2t[:, :, :, :].rearrange("p j b c -> p (j b c)"), X2T).then_inc(s["x2t_ready"], 1)
            act.wait_ge(s["negmax_ready"], 1)
            nc.scalar.activation(gexp[:, :], logit[:, :], ACT.Exp, bias=negmax[:, :],
                                 accum_out=gsum[:, :]).then_inc(s["gexp_ready"], 1)
            nc.scalar.preload_act_table(ACT.Gelu)
            act.wait_ge(s["h_mm"], 1)
            act.wait_ge(s["hdiag_zero"], 1)
            hd = hdiag[:, :, :]
            place = bass.AP(hd.tensor, hd.offset, [list(hd.ap[0]), [P + GE, NG], [1, GE], [EP, B]])
            nc.scalar.activation(place, HH.rearrange("p (g e b) -> p g e b", g=NG, e=GE),
                                 ACT.Gelu).then_inc(s["h_ready"], 1)
            act.wait_ge(s["f_mm"], 2)
            nc.scalar.copy(fin[:, P:2 * P], T[1]).then_inc(s["final_act"], 1)
            act.wait_ge(s["final_act"], 1)
            act.dma_start(out[:, P:2 * P], fin[:, P:2 * P]).then_inc(s["out_done"], 16)

        @block.vector
        def _(dve):
            dve.wait_ge(s["x_in"], 16)
            nc.vector.bn_stats(bst[:, :], xs[:, :]).then_inc(s["stats"], 1)
            dve.wait_ge(s["stats"], 1)
            nc.vector.bn_aggr(bag[:, :], bst[:, :]).then_inc(s["agg"], 1)
            dve.wait_ge(s["rstd"], 1)
            dve.wait_ge(s["wqkv_in"], 16)
            nc.vector.tensor_tensor(sca[:, :], rstd[:, :], v["in_gamma"], ALU.mult).then_inc(s["scale"], 1)
            dve.wait_ge(s["scale"], 1)
            nc.vector.scalar_tensor_tensor(shi[:, :], bag[:, 0:1], sca[:, :], v["in_beta"],
                                           ALU.mult, ALU.subtract).then_inc(s["shift"], 1)
            dve.wait_ge(s["shift"], 1)
            nc.vector.tensor_scalar(xn[:, :], xs[:, :], sca[:, :], shi[:, :],
                                    ALU.mult, ALU.subtract).then_inc(s["xn_ready"], 1)
            dve.wait_ge(s["q_mm"], 1)
            dve.wait_ge(s["qm_zero"], 1)
            for b in range(B):
                nc.vector.tensor_scalar(img(qm[:, b, :], b), img(Q, b), img(v["bq"], b), float(C) ** -0.5,
                                        ALU.add, ALU.mult).then_inc(s["q_dve"], 1)

            def take_max(b):
                dve.wait_ge(s["s_mm"], b + 1)
                nc.vector.tensor_reduce(nmx[:, b, :], bank(b).rearrange("p (j m) -> p j m", j=J),
                                        AX.X, ALU.max, negate=True).then_inc(s["max_ready"], 1)

            def take_pt(b):
                dve.wait_ge(s["pt_mm"], b + 1)
                nc.vector.tensor_copy(pt[:, b, :, :].rearrange("p i n -> p (i n)"), bank(4 + b))\
                    .then_inc(s["pt_dve"], 1)

            take_max(0)
            take_max(1)
            take_max(2)
            take_pt(0)
            take_max(3)
            take_pt(1)
            take_pt(2)
            dve.wait_ge(s["exp_ready"], J * B)
            nc.vector.reciprocal(rs[:, :, :], rsum[:, :, :]).then_inc(s["rsum_ready"], 1)
            dve.wait_ge(s["pv_mm"], B)
            dve.wait_ge(s["rsum_ready"], 1)
            rsb = rs[:, :, :].unsqueeze(3).to_broadcast([P, J, B, C])
            for kind, done in ((1, s["onu_ready"]), (0, s["ono_ready"])):
                nc.vector.tensor_tensor(on[:, kind, :, :].rearrange("p j (b c) -> p j b c", b=B),
                                        O[:, :, :, kind * C:(kind + 1) * C], rsb, ALU.mult).then_inc(done, 1)
            dve.wait_ge(s["u_mm"], 1)
            nc.vector.bn_stats(ubst[:, :], U).then_inc(s["ustats"], 1)
            dve.wait_ge(s["ustats"], 1)
            nc.vector.bn_aggr(ubag[:, :], ubst[:, :]).then_inc(s["uagg"], 1)
            dve.wait_ge(s["urstd"], 1)
            nc.vector.tensor_tensor(usca[:, :], urstd[:, :], v["g_cbr"], ALU.mult).then_inc(s["uscale"], 1)
            dve.wait_ge(s["uscale"], 1)
            nc.vector.scalar_tensor_tensor(ushi[:, :], ubag[:, 0:1], usca[:, :], v["be_cbr"],
                                           ALU.mult, ALU.subtract).then_inc(s["ushift"], 1)
            dve.wait_ge(s["ushift"], 1)
            nc.vector.tensor_scalar(uaff[:, :], U, usca[:, :], ushi[:, :],
                                    ALU.mult, ALU.subtract).then_inc(s["uaff"], 1)
            dve.wait_ge(s["uaff"], 1)
            dve.wait_ge(s["o_mm"], 1)
            nc.vector.scalar_tensor_tensor(y[:, :], uaff[:, :], 0.0, OO, ALU.max, ALU.add)\
                .then_inc(s["y_ready"], 1)
            dve.wait_ge(s["ysq_ready"], 1)
            nc.vector.tensor_reduce(yvar[:, :, :], ysq[:, :, :, :], AX.X, ALU.add).then_inc(s["yvar_ready"], 1)
            dve.wait_ge(s["yrstd_ready"], 1)
            nc.vector.tensor_tensor(xt[:, :, :, :], YC, yrstd[:, :, :].unsqueeze(3).to_broadcast([P, J, B, C]),
                                    ALU.mult).then_inc(s["xt_ready"], 1)
            dve.wait_ge(s["g_mm"], 1)
            dve.wait_ge(s["cons_in"], 16)
            nc.vector.tensor_tensor(gbd[:, :], G, c["block"], ALU.mult).then_inc(s["g_ready"], 1)
            dve.wait_ge(s["tsq_ready"], 1)
            nc.vector.tensor_copy(tcs[:, :], TC).then_inc(s["tcs_ready"], 1)
            dve.wait_ge(s["trstd_ready"], 1)
            dve.wait_ge(s["raw_mm"], 1)
            nc.vector.tensor_tensor(logit[:, :], RAW, trstd[:, :], ALU.mult).then_inc(s["logits_ready"], 1)
            dve.wait_ge(s["logits_ready"], 1)
            nc.vector.max(top[:, :], logit[:, :]).then_inc(s["top_ready"], 1)
            dve.wait_ge(s["top_ready"], 1)
            nc.vector.scalar_tensor_tensor(negmax[:, :], top[:, 0:1], v["gate_b"], v["gate_b"], ALU.add,
                                           ALU.subtract, reverse1=True).then_inc(s["negmax_ready"], 1)
            nc.vector.match_replace(taken[:, :], top[:, :], logit[:, :], TAKEN).then_inc(s["taken_ready"], 1)
            dve.wait_ge(s["taken_ready"], 1)
            dve.wait_ge(s["gexp_ready"], 1)
            nc.vector.scalar_tensor_tensor(wm[:, :], taken[:, :], TAKEN, gexp[:, :],
                                           ALU.is_equal, ALU.mult).then_inc(s["wm_ready"], 1)
            nc.vector.reciprocal(grec[:, :], gsum[:, :]).then_inc(s["grec_ready"], 1)
            dve.wait_ge(s["wt_mm"], 1)
            nc.vector.tensor_copy(wt[:, :, :, :].rearrange("p j b e -> p (j b e)"), WT).then_inc(s["wt_ready"], 1)
            dve.wait_ge(s["pool_mm"], 1)
            dve.wait_ge(s["grec_ready"], 1)
            nc.vector.tensor_scalar(rep[:, :, :], POOL.unsqueeze(1).to_broadcast([P, GE, C]), grec[:, :], None,
                                    ALU.mult).then_inc(s["rep_ready"], 1)
            dve.wait_ge(s["rept_mm"], 1)
            dve.wait_ge(s["masks_in"], 16)
            nc.vector.tensor_tensor(pooled[:, :, :, :],
                                    REPT.rearrange("p (b e) -> p b e", b=B)[:, :, 0:E]
                                    .rearrange("p b (g e) -> p g e b", g=NG),
                                    msk[:, 0:E * B].rearrange("p (g e b) -> p g e b", g=NG, e=GE),
                                    ALU.mult).then_inc(s["pool_ready"], 1)
            dve.wait_ge(s["z_mm"], 1)
            nc.vector.scalar_tensor_tensor(zsel[:, :, :], Z.rearrange("p (e c) -> p e c", e=GE), grec[:, :],
                                           msk[:, E * B:].unsqueeze(2).to_broadcast([P, GE, C]),
                                           ALU.mult, ALU.mult).then_inc(s["zsel_ready"], 1)
            dve.wait_ge(s["zsel_ready"], 1)
            nc.vector.tensor_reduce(zsum[:, :], zsel[:, :, :].rearrange("p e c -> p c e"), AX.X, ALU.add)\
                .then_inc(s["zsum_ready"], 1)
            dve.wait_ge(s["zsum_ready"], 1)
            nc.vector.tensor_tensor(zbd[:, :, :], zsum[:, :].unsqueeze(1).to_broadcast([P, B, C]),
                                    c["block"].rearrange("p (b c) -> p b c", b=B), ALU.mult)\
                .then_inc(s["z_ready"], 1)
            dve.wait_ge(s["f_mm"], 1)
            nc.vector.tensor_copy(fin[:, 0:P], T[0]).then_inc(s["final_dve"], 1)

        @block.tensor
        def _(pe):
            mm = nc.tensor.matmul

            def keep_warm(n):
                for _ in range(n):
                    mm(IDLE, warm[:, 0:P], warm[:, :], start=True, stop=True)

            pe.wait_ge(s["warm_set"], 1)
            keep_warm(WARM[0])
            pe.wait_ge(s["xn_ready"], 1)
            pe.wait_ge(s["wqkv_in"], 16)
            mm(Q, wqT, xn[:, :], start=True, stop=True).then_inc(s["q_mm"], 1)
            mm(KK, wkT, xn[:, :], start=True, stop=True).then_inc(s["k_mm"], 1)
            pe.wait_ge(s["wvo_in"], 16)
            mm(PROD1[:, 0:P], m["woT"], m["wv"], start=True, stop=True)
            mm(PROD1[:, P:2 * P], m["wv"], m["woT"], start=True, stop=True).then_inc(s["prod1_mm"], 1)

            def scores(b):
                pe.wait_ge(s["q_dve"], b + 1)
                for j in range(J):
                    last = mm(bank(b, N, j * N), chunk(qm[:, b, :], j), k[:, :], start=True, stop=True)
                last.then_inc(s["s_mm"], 1)

            def transposes(b):
                pe.wait_ge(s["exp_ready"], J * (b + 1))
                for j in range(J):
                    for i in range(J):
                        last = nc.tensor.transpose(bank(4 + b, P, i * N + j * P), chunk(prob[:, b, j, :], i),
                                                   c["ident"])
                last.then_inc(s["pt_mm"], 1)

            def attend(b):
                if b < B - 1:
                    pe.wait_ge(s["pt_dve"], b + 1)
                else:
                    pe.wait_ge(s["pt_act"], 1)
                for j in range(J):
                    for i in range(J):
                        last = mm(O[:, j, b, :], chunk(pt[:, b, i, :], j), vt[:, i, b, :],
                                  start=(i == 0), stop=(i == J - 1))
                last.then_inc(s["pv_mm"], 1)

            pe.wait_ge(s["k_ready"], 1)
            scores(0)
            pe.wait_ge(s["prod1_ready"], 1)
            mm(PROD2, prod1[:, :], m["wcT"], start=True, stop=True)
            mm(BIAS1, m["woT"], v["bv"], start=True, stop=True).then_inc(s["prod2_mm"], 1)
            scores(1)
            pe.wait_ge(s["prod1_ready"], 2)
            pe.wait_ge(s["prod2_ready"], 1)
            for i in range(J):
                last = mm(V[:, i, :, :, :].rearrange("p k b c -> p (k b c)"), chunk(xn, i),
                          vmat[:, :, :].rearrange("p k c -> p (k c)"), start=True, stop=True)
            last.then_inc(s["v_mm"], 1)
            scores(2)
            pe.wait_ge(s["cons_in"], 16)
            transposes(0)
            pe.wait_ge(s["bias1_ready"], 1)
            scores(3)
            transposes(1)
            pe.wait_ge(s["v_ready"], J)
            attend(0)
            pe.wait_ge(s["xres_ready"], 1)
            pe.wait_ge(s["rows_in"], 16)
            pe.wait_ge(s["ones_set"], 1)
            mm(U, m["wcT"], xres[:, :], start=True, stop=False, skip_group_check=True)
            mm(U, row[0:1, 1, 0:P], ones[:, :], start=False, stop=False, skip_group_check=True)
            transposes(2)
            attend(1)
            mm(OO, c["ident"], xres[:, :], start=True, stop=False, skip_group_check=True)
            transposes(3)
            attend(2)
            attend(3)
            keep_warm(WARM[1])
            for kind, acc, ready, done in ((1, U, s["onu_ready"], s["u_mm"]), (0, OO, s["ono_ready"], s["o_mm"])):
                pe.wait_ge(ready, 1)
                for j in range(J):
                    last = mm(chunk(acc, j), on[:, kind, j, :], c["ident"],
                              start=False, stop=True, skip_group_check=True)
                last.then_inc(done, 1)
            keep_warm(WARM[2])
            pe.wait_ge(s["y_ready"], 1)
            for j in range(J):
                last = mm(YC[:, j, :, :].rearrange("p b c -> p (b c)"), chunk(y, j), c["center"],
                          start=True, stop=True)
            last.then_inc(s["yc_mm"], 1)
            mm(TC, c["center"], y[:, :], start=True, stop=False, skip_group_check=True)
            for j in range(J):
                mm(T[j], c["ident"], chunk(y, j), start=True, stop=False, skip_group_check=True)
            keep_warm(WARM[3])
            pe.wait_ge(s["xt_ready"], 1)
            xtj = [xt[:, j, :, :].rearrange("p b c -> p (b c)") for j in range(J)]
            for j in range(J):
                last = mm(G, xtj[j], xtj[j], start=(j == 0), stop=(j == J - 1))
            last.then_inc(s["g_mm"], 1)
            for j in range(J):
                last = nc.tensor.transpose(chunk(XC, j), xtj[j], c["ident"])
            last.then_inc(s["xc_mm"], 1)
            keep_warm(WARM[4])
            pe.wait_ge(s["g_ready"], 1)
            pe.wait_ge(s["xc_ready"], 1)
            mm(TC, gbd[:, :], xc[:, :], start=False, stop=True, skip_group_check=True).then_inc(s["tc_mm"], 1)
            keep_warm(WARM[5])
            pe.wait_ge(s["tsq_ready"], 1)
            mm(VAR, c["mean"], tsq[:, :], start=True, stop=True).then_inc(s["var_mm"], 1)
            pe.wait_ge(s["tcs_ready"], 1)
            mm(RAW, m["gateT"], tcs[:, :], start=True, stop=True).then_inc(s["raw_mm"], 1)
            for j in range(J):
                mm(T[j], gbd[:, :], chunk(xc, j), start=False, stop=False, skip_group_check=True)
            mm(HH, row[:, 0, 0:H], row[:, 2, 0:E * B], start=True, stop=False, skip_group_check=True)
            mm(Z, row[:, 3, 0:P], row[:, 1, P:P + C].unsqueeze(1).to_broadcast([E, GE, C]), start=True,
               stop=False, skip_group_check=True)
            keep_warm(WARM[6])
            pe.wait_ge(s["x2c_ready"], 1)
            for j in range(J):
                last = nc.tensor.transpose(chunk(X2T, j), chunk(x2c, j), c["ident"])
            last.then_inc(s["x2t_mm"], 1)
            keep_warm(WARM[7])
            pe.wait_ge(s["wm_ready"], 1)
            for j in range(J):
                last = nc.tensor.transpose(chunk(WT, j), chunk(wm, j), c["ident"])
            last.then_inc(s["wt_mm"], 1)
            keep_warm(WARM[8])
            pe.wait_ge(s["wt_ready"], 1)
            pe.wait_ge(s["x2t_ready"], 1)
            for b in range(B):
                for j in range(J):
                    last = mm(img(POOL, b), wt[:, j, b, :], x2t[:, j, b, :], start=(j == 0), stop=(j == J - 1))
            last.then_inc(s["pool_mm"], 1)
            keep_warm(WARM[9])
            pe.wait_ge(s["rep_ready"], 1)
            nc.tensor.transpose(REPT, rep[:, :, :].rearrange("p g c -> p (g c)"), c["ident"])\
                .then_inc(s["rept_mm"], 1)
            keep_warm(WARM[9])
            pe.wait_ge(s["pool_ready"], 1)
            pe.wait_ge(s["w1_in"], 16)
            for g in range(NG):
                last = mm(HH[:, g * GE * B:(g + 1) * GE * B], w1s[:, g, :],
                          pooled[:, g, :, :].rearrange("p e b -> p (e b)"),
                          start=False, stop=True, skip_group_check=True)
            last.then_inc(s["h_mm"], 1)
            keep_warm(WARM[10])
            pe.wait_ge(s["h_ready"], 1)
            pe.wait_ge(s["w2_in"], 16)
            for g in range(NG):
                last = mm(Z, hdiag[:, g, :], w2s[:, g * GE:(g + 1) * GE, :].rearrange("p e c -> p (e c)"),
                          start=False, stop=(g == NG - 1), skip_group_check=True)
            last.then_inc(s["z_mm"], 1)
            keep_warm(WARM[11])
            pe.wait_ge(s["z_ready"], 1)
            for j in range(J):
                mm(T[j], zbd[:, :, :].rearrange("p b c -> p (b c)"), chunk(wm, j),
                   start=False, stop=True, skip_group_check=True).then_inc(s["f_mm"], 1)


def kernel(**inputs):
    import concourse.bacc as bacc
    from concourse.bass_utils import run_bass_kernel_spmd

    a = {n: np.asarray(t) for n, t in inputs.items()}
    f = np.float32

    def tiled(t):
        return np.tile(t, B)

    def diagonal(t):
        d = np.zeros((B, C, B, t.shape[1]), f)
        for b in range(B):
            d[b, :, b, :] = t
        return d.reshape(P, -1)

    L = "L0_conv_"
    gate_b = np.zeros(EP, f)
    gate_b[:E] = a["L1_ffn_gate_b"]
    cols = [a[L + n] for n in VEC[:-1]] + [gate_b]
    vecs = np.stack([tiled(t) for t in cols], axis=1)

    gateT = np.zeros((C, EP), f)
    gateT[:, :E] = a["L1_ffn_gate_w"].T
    wqkv = np.concatenate([diagonal(a[L + "wq"].T), diagonal(a[L + "wk"].T), vecs], axis=1)
    mats = np.stack([diagonal(t) for t in (a[L + "wv"], a[L + "wo"].T,
                                           a[L + "w_cbr"].T, gateT)], axis=1)

    blk = diagonal(np.ones((C, C), f))
    cons = np.stack([np.eye(P, dtype=f), np.eye(P, dtype=f) - blk / f(C), blk / f(C), blk], axis=1)
    masks = np.zeros((P, E * B + GE), f)
    masks[:, :E * B] = np.broadcast_to(np.eye(GE, dtype=f)[:, None, None, :, None],
                                     (GE, C, NG, GE, B)).reshape(P, E * B)
    for b in range(B):
        masks[b * EP:b * EP + E, E * B:] = np.tile(np.eye(GE, dtype=f), (NG, 1))

    w1, w2 = a["L1_ffn_weight1"], a["L1_ffn_weight2"]
    w1g = np.ascontiguousarray(w1[:, :C, :].reshape(NG, GE, C, H).transpose(1, 2, 0, 3).reshape(P, NG, H))
    w2g = np.ascontiguousarray(w2[:, :H, :].transpose(1, 0, 2))
    rows = np.zeros((E, 4, P + C), f)
    rows[:, 0, :H] = w1[:, C, :]
    rows[0, 1, :P] = tiled(a[L + "b_cbr"])
    rows[:, 1, P:] = w2[:, H, :]
    rows[:, 2, :E * B] = np.repeat(np.eye(E, dtype=f), B, axis=1)
    for b in range(B):
        rows[:, 3, b * EP:b * EP + E] = np.eye(E, dtype=f)

    arrays = {"x": np.ascontiguousarray(a["x"].reshape(P, N)), "wqkv": wqkv, "mats": mats, "cons": cons,
              "masks": masks, "w1": w1g, "w2": w2g, "rows": rows}
    nc = bacc.Bacc("TRN2", target_bir_lowering=False, num_devices=1)
    args = [nc.dram_tensor(n, t.shape, F32, kind="ExternalInput").ap() for n, t in arrays.items()]
    args.append(nc.dram_tensor("out", (P, N), F32, kind="ExternalOutput").ap())
    hybrid_block(nc, *args)
    r = run_bass_kernel_spmd(nc, [arrays], core_ids=[0])
    return r.results[0]["out"].reshape(B, C, 16, 16)
```

```python
from contextlib import ExitStack

import numpy as np

import concourse.bass as bass
from concourse import mybir

F32 = mybir.dt.float32
ALU = mybir.AluOpType
ACT = mybir.ActivationFunctionType
AX = mybir.AxisListType

B, C, N = 4, 32, 256
P = B * C
J = N // P
E, H, K = 16, 128, 8
EP = 32
GE = P // C
NG = E // GE
EPS = 1e-5
TAKEN = -3.0e38
WARM = {"load": 14, "y": 6, "yw": 4, "x2c": 6, "wm": 8, "wt": 4, "rep": 2, "h": 1, "z": 6}

VEC = ["in_gamma", "in_beta", "bq", "bk", "bv", "bo", "g_cbr", "be_cbr", "gate_b"]
MAT = ["wv", "woT", "wcT"]
CON = ["ident", "center", "mean", "block", "gateT"]


def hybrid_block(nc, xv, wqk, mats, bcb, cons, masks, w1, w2, rows, out):
    with ExitStack() as ctx:
        def sb(name, shape):
            return ctx.enter_context(nc.sbuf_tensor(name, shape, F32))

        names = """x_in wqk_in wvo_in cons_in masks_in w1_in w2_in rows_in bcbr_in out_done
            eps_set ysq_eps hdiag_zero qm_zero
            stats agg lnv rstd xcen_ready xn_ready
            prod1_mm vmat0_mm prod1_ready vmat0_ready prod2_mm prod2_ready bias1_mm bias1_ready xres_ready
            q_mm k_mm q_ready k_ready v_mm vu_ready vo_ready
            s_mm max_ready exp_ready pt_mm pt_dve pt_act pv_mm pv0_mm rsum_ready
            onu_ready ono_ready u_mm o_mm ustats uagg lnu urstd ucen_ready uaff urelu y_ready
            yc_mm ysq_ready yvar_ready ycs_ready yr2_ready yw_ready lny yrstd_ready xt_ready g_mm g_ready xc_mm xc_ready
            tc_mm tsq_ready tcs_ready var_mm raw_mm lnt trstd_ready logits_ready
            x2c_ready x2t_mm x2t_ready top_ready negmax_ready gexp_ready gsum_ready taken_ready
            wm_ready grec_ready wt_mm wt_dve wt_act pool_mm rep_ready rept_mm pool_ready h_mm h_ready
            z_mm place_ready zsel_ready zsum_ready z_ready f_mm final_dve final_act"""
        s = {n: ctx.enter_context(nc.semaphore(n)) for n in names.split()}

        ps = ctx.enter_context(nc.psum_tensor("ps", [P, 8, 512], F32))

        xvec = sb("xvec", [P, N + len(VEC)])
        xs = xvec[:, 0:N]
        qkv = sb("qkv", [P, 2, P])
        mat = sb("mat", [P, len(MAT), P])
        con = sb("con", [P, len(CON), P])
        v = {n: xvec[:, N + i:N + i + 1] for i, n in enumerate(VEC)}
        m = {n: mat[:, i, :] for i, n in enumerate(MAT)} | {"wqT": qkv[:, 0, :], "wkT": qkv[:, 1, :]}
        c = {n: con[:, i, :] for i, n in enumerate(CON)}
        msk = sb("msk", [P, E * B + GE])
        w1s = sb("w1s", [P, NG, H])
        w2s = sb("w2s", [P, E, C])
        row = sb("row", [E, 4, P])
        bcbr = sb("bcbr", [P, P])
        idle = nc.const_aps.tensor(1.0, [P, 2 * P], mybir.dt.bfloat16)
        eps = sb("eps", [P, P])

        bst, bag = sb("bst", [P, 6]), sb("bag", [P, 2])
        rstd, xcen = sb("rstd", [P, 1]), sb("xcen", [P, N])
        xn = sb("xn", [P, N])
        prod1 = sb("prod1", [P, P])
        vmat = sb("vmat", [P, 2, P])
        bias1 = sb("bias1", [P, 1])
        xres = sb("xres", [P, N])
        qm = sb("qm", [P, B, N])
        k = sb("k", [P, N])
        vt = sb("vt", [P, J, B, 2 * C])
        nmx, rsum = sb("nmx", [P, B, J]), sb("rsum", [P, J, B])
        prob = sb("prob", [P, B, J, N])
        pt = sb("pt", [P, B, J, N])
        rs = sb("rs", [P, J, B])
        on = sb("on", [P, 2, J, P])
        ubst, ubag = sb("ubst", [P, J, 6]), sb("ubag", [P, 2])
        urstd, ucen = sb("urstd", [P, 1]), sb("ucen", [P, J, P])
        uaff = sb("uaff", [P, J, P])
        y = sb("y", [P, N])
        ysq = sb("ysq", [P, J, B, C + 1])
        ycs, yw, yr2 = sb("ycs", [P, J, B, C]), sb("yw", [P, J, B, C]), sb("yr2", [P, J, B])
        yvar, yrstd = sb("yvar", [P, J, B]), sb("yrstd", [P, J, B])
        xt = sb("xt", [P, J, B, C])
        gbd = sb("gbd", [P, P])
        xc = sb("xc", [P, N])
        tsq, tcs = sb("tsq", [P, N]), sb("tcs", [P, N])
        trstd, logit = sb("trstd", [P, N]), sb("logit", [P, N])
        x2c = sb("x2c", [P, N])
        x2t = sb("x2t", [P, J, B, C])
        top, negmax, gsum, grec = sb("top", [P, K]), sb("negmax", [P, 1]), sb("gsum", [P, 1]), sb("grec", [P, 1])
        gcopy = sb("gcopy", [P, N])
        gexp, taken, wm = sb("gexp", [P, N]), sb("taken", [P, N]), sb("wm", [P, N])
        wt = sb("wt", [P, J, B, EP])
        rep = sb("rep", [P, GE, C])
        pooled = sb("pooled", [P, NG, GE, B])
        hdiag = sb("hdiag", [P, NG, P])
        place = sb("place", [P, GE])
        zsel, zsum = sb("zsel", [P, GE, C]), sb("zsum", [P, C])
        zbd = sb("zbd", [P, B, C])
        fin = sb("fin", [P, N])

        def bank(i, n=512, at=0):
            return ps[:, i, at:at + n]

        def img(t, b):
            return t[b * C:(b + 1) * C, :]

        def chunk(t, j):
            return t[:, j * P:(j + 1) * P]

        SCORES, PT = [0, 1, 2, 6], [4, 5, 2, 7]
        Q, KK = bank(4, N), bank(5, N)
        PROD1, VO, PROD2, BIAS1 = bank(6, P), bank(1, P), bank(3, P), bank(2, 1)
        V = bank(7).rearrange("p (i k b c) -> p i k b c", i=J, k=2, b=B)
        O = [[bank(j, (B - 1) * 2 * C), bank([5, 2][j], 2 * C)] for j in range(J)]
        O = [[o.rearrange("p (b c) -> p b c", c=2 * C) for o in oj] for oj in O]
        U, OO = ps[:, 3:3 + J, 0:P], bank(6, N)
        YC = ps[:, 5:5 + J, 0:P].rearrange("p j (b c) -> p j b c", b=B)
        G, XC, TC = bank(2, P), [bank(4, P), bank(6, P)], [bank(7, P), bank(3, P)]
        LNV, LNU, LNY = bank(7, 1), bank(7, 1), bank(4, J * B).rearrange("p (j b) -> p j b", j=J)
        T = ps[:, 0:J, 0:P]
        VAR, RAW, X2T = [bank(5, P), bank(2, P)], bank(4, N), bank(6, N)
        WT = ps[:, 5:5 + J, 0:P]
        POOL, REPT, Z = bank(4, C), bank(6, P), bank(7, GE * C)
        HH = [bank(2, E * B // 2), bank(5, E * B // 2)]

        block = ctx.enter_context(nc.Block())

        @block.sync
        def _(sp):
            sp.dma_start(xvec[:, :], xv).then_inc(s["x_in"], 16)
            sp.dma_start(mat[:, :, :], mats).then_inc(s["wvo_in"], 16)
            sp.dma_start(qkv[:, :, :], wqk).then_inc(s["wqk_in"], 16)
            sp.dma_start(con[:, :, :], cons).then_inc(s["cons_in"], 16)
            sp.dma_start(bcbr[:, :], bcb).then_inc(s["bcbr_in"], 16)
            sp.dma_start(row[:, :, :], rows).then_inc(s["rows_in"], 16)
            sp.dma_start(msk[:, :], masks).then_inc(s["masks_in"], 16)
            sp.dma_start(w1s[:, :, :], w1).then_inc(s["w1_in"], 16)
            sp.dma_start(w2s[:, :, :], w2).then_inc(s["w2_in"], 16)
            sp.wait_ge(s["final_act"], 1)
            sp.wait_ge(s["final_dve"], 1)
            sp.dma_start(out, fin[:, :]).then_inc(s["out_done"], 16)
            sp.wait_ge(s["out_done"], 16)

        @block.gpsimd
        def _(pool):
            nc.gpsimd.memset(eps[:, :], EPS).then_inc(s["eps_set"], 1)
            nc.gpsimd.memset(ysq[:, :, :, C:], EPS).then_inc(s["ysq_eps"], 1)
            nc.gpsimd.memset(qm[:, :, :], 0.0).then_inc(s["qm_zero"], 1)
            nc.gpsimd.memset(hdiag[:, :, :], 0.0).then_inc(s["hdiag_zero"], 1)
            pool.wait_ge(s["trstd_ready"], J)
            pool.wait_ge(s["tcs_ready"], J)
            nc.gpsimd.tensor_tensor(x2c[:, :], tcs[:, :], trstd[:, :], ALU.mult).then_inc(s["x2c_ready"], 1)

        @block.scalar
        def _(act):
            nc.scalar.preload_act_table_set("natural_log_exp_and_others")

            def rsqrt(dst, var, log, logged, done, bias=eps[:, 0:1]):
                nc.scalar.activation(log, var, ACT.Ln, bias=bias).then_inc(logged, 1)
                act.wait_ge(logged, 1)
                nc.scalar.activation(dst, log, ACT.Exp, scale=-0.5).then_inc(done, 1)

            act.wait_ge(s["agg"], 1)
            act.wait_ge(s["eps_set"], 1)
            rsqrt(rstd[:, :], bag[:, 1:2], LNV, s["lnv"], s["rstd"])
            act.wait_ge(s["prod1_mm"], 1)
            nc.scalar.copy(prod1[:, :], PROD1).then_inc(s["prod1_ready"], 1)
            act.wait_ge(s["vmat0_mm"], 1)
            nc.scalar.copy(vmat[:, 0, :], VO).then_inc(s["vmat0_ready"], 1)
            act.wait_ge(s["prod2_mm"], 1)
            nc.scalar.copy(vmat[:, 1, :], PROD2).then_inc(s["prod2_ready"], 1)
            act.wait_ge(s["k_mm"], 1)
            nc.scalar.activation(k[:, :], KK, ACT.Identity, bias=v["bk"]).then_inc(s["k_ready"], 1)
            act.wait_ge(s["bias1_mm"], 1)
            nc.scalar.activation(bias1[:, :], BIAS1, ACT.Identity, bias=v["bo"]).then_inc(s["bias1_ready"], 1)
            act.wait_ge(s["bias1_ready"], 1)
            nc.scalar.activation(xres[:, :], xs[:, :], ACT.Identity, bias=bias1[:, :]).then_inc(s["xres_ready"], 1)
            for b in range(B):
                act.wait_ge(s["max_ready"], b + 1)
                for j in range(J):
                    nc.scalar.activation(prob[:, b, j, :], bank(SCORES[b], N, j * N), ACT.Exp, bias=nmx[:, b, j:j + 1],
                                         accum_out=rsum[:, j, b:b + 1]).then_inc(s["exp_ready"], 1)
                if b == 0 and j == J - 1:
                    act.wait_ge(s["vu_ready"], 1)
                    nc.scalar.copy(vt[:, :, :, 0:C], V[:, :, 0, :, :]).then_inc(s["vo_ready"], 1)
            act.wait_ge(s["pt_mm"], B)
            nc.scalar.copy(pt[:, B - 1, :, :].rearrange("p i n -> p (i n)"), bank(PT[B - 1])).then_inc(s["pt_act"], 1)
            act.wait_ge(s["uagg"], 1)
            rsqrt(urstd[:, :], ubag[:, 1:2], LNU, s["lnu"], s["urstd"])
            act.wait_ge(s["ucen_ready"], 1)
            act.wait_ge(s["urstd"], 1)
            nc.scalar.activation(uaff[:, 1, :], ucen[:, 1, :], ACT.Relu, scale=urstd[:, :],
                                 bias=v["be_cbr"]).then_inc(s["urelu"], 1)
            for j in range(J):
                act.wait_ge(s["yc_mm"], j + 1)
                nc.scalar.activation(ysq[:, j, :, 0:C], YC[:, j, :, :], ACT.Square, scale=float(C) ** -0.5)\
                    .then_inc(s["ysq_ready"], 1)
            for j in range(J):
                nc.scalar.copy(ycs[:, j, :, :], YC[:, j, :, :]).then_inc(s["ycs_ready"], 1)
            act.wait_ge(s["yvar_ready"], J)
            rsqrt(yrstd[:, :, :], yvar[:, :, :], LNY, s["lny"], s["yrstd_ready"], bias=0.0)
            for j in range(J):
                act.wait_ge(s["xc_mm"], j + 1)
                nc.scalar.copy(chunk(xc, j), XC[j]).then_inc(s["xc_ready"], 1)
            for j in range(J):
                act.wait_ge(s["tc_mm"], j + 1)
                nc.scalar.activation(chunk(tsq, j), TC[j], ACT.Square).then_inc(s["tsq_ready"], 1)
            for j in range(J):
                act.wait_ge(s["var_mm"], j + 1)
                nc.scalar.activation(VAR[j], VAR[j], ACT.Ln).then_inc(s["lnt"], 1)
            for j in range(J):
                act.wait_ge(s["lnt"], j + 1)
                nc.scalar.activation(chunk(trstd, j), VAR[j], ACT.Exp, scale=-0.5)\
                    .then_inc(s["trstd_ready"], 1)
            act.wait_ge(s["negmax_ready"], 1)
            nc.scalar.activation(gexp[:, :], logit[:, :], ACT.Exp, bias=negmax[:, :]).then_inc(s["gexp_ready"], 1)
            act.wait_ge(s["x2t_mm"], 1)
            nc.scalar.copy(x2t[:, :, :, :].rearrange("p j b c -> p (j b c)"), X2T).then_inc(s["x2t_ready"], 1)
            act.wait_ge(s["gexp_ready"], 1)
            nc.scalar.activation(gcopy[:, :], gexp[:, :], ACT.Copy, accum_out=gsum[:, :]).then_inc(s["gsum_ready"], 1)
            act.wait_ge(s["wt_mm"], 2)
            nc.scalar.copy(wt[:, 1, :, :].rearrange("p b e -> p (b e)"), WT[:, 1, :]).then_inc(s["wt_act"], 1)
            nc.scalar.preload_act_table(ACT.Gelu)
            hd = hdiag[:, :, :]
            for half in range(2):
                act.wait_ge(s["h_mm"], half + 1)
                if half == 0:
                    act.wait_ge(s["hdiag_zero"], 1)
                columns = bass.AP(hd.tensor, hd.offset + half * (NG // 2) * (P + GE),
                                  [list(hd.ap[0]), [P + GE, NG // 2], [1, GE], [EP, B]])
                nc.scalar.activation(columns, HH[half].rearrange("p (g e b) -> p g e b", e=GE, b=B),
                                     ACT.Gelu).then_inc(s["h_ready"], 1)
            act.wait_ge(s["f_mm"], 2)
            nc.scalar.copy(fin[:, P:2 * P], T[:, 1, :]).then_inc(s["final_act"], 1)

        @block.vector
        def _(dve):
            dve.wait_ge(s["x_in"], 16)
            nc.vector.bn_stats(bst[:, :], xs[:, :]).then_inc(s["stats"], 1)
            dve.wait_ge(s["stats"], 1)
            nc.vector.bn_aggr(bag[:, :], bst[:, :]).then_inc(s["agg"], 1)
            dve.wait_ge(s["agg"], 1)
            nc.vector.tensor_scalar(xcen[:, :], xs[:, :], bag[:, 0:1], v["in_gamma"],
                                    ALU.subtract, ALU.mult).then_inc(s["xcen_ready"], 1)
            dve.wait_ge(s["rstd"], 1)
            dve.wait_ge(s["xcen_ready"], 1)
            nc.vector.tensor_scalar(xn[:, :], xcen[:, :], rstd[:, :], v["in_beta"],
                                    ALU.mult, ALU.add).then_inc(s["xn_ready"], 1)
            dve.wait_ge(s["q_mm"], 1)
            dve.wait_ge(s["qm_zero"], 1)
            for b in range(B):
                nc.vector.tensor_scalar(img(qm[:, b, :], b), img(Q, b), img(v["bq"], b), float(C) ** -0.5,
                                        ALU.add, ALU.mult).then_inc(s["q_ready"], 1)

            def take_max(b):
                dve.wait_ge(s["s_mm"], b + 1)
                nc.vector.tensor_reduce(nmx[:, b, :], bank(SCORES[b]).rearrange("p (j m) -> p j m", j=J),
                                        AX.X, ALU.max, negate=True).then_inc(s["max_ready"], 1)

            def take_pt(b):
                dve.wait_ge(s["pt_mm"], b + 1)
                nc.vector.tensor_copy(pt[:, b, :, :].rearrange("p i n -> p (i n)"), bank(PT[b]))\
                    .then_inc(s["pt_dve"], 1)

            take_max(0)
            dve.wait_ge(s["v_mm"], 1)
            dve.wait_ge(s["bcbr_in"], 16)
            nc.vector.tensor_tensor(vt[:, :, :, C:2 * C], V[:, :, 1, :, :],
                                    bcbr[:, :].rearrange("p (b c) -> p b c", b=B).unsqueeze(1)
                                    .to_broadcast([P, J, B, C]), ALU.add).then_inc(s["vu_ready"], 1)
            take_max(1)
            take_max(2)
            take_pt(0)
            take_max(3)
            take_pt(1)
            take_pt(2)
            dve.wait_ge(s["exp_ready"], J * B)
            nc.vector.reciprocal(rs[:, :, :], rsum[:, :, :]).then_inc(s["rsum_ready"], 1)

            def normalise(kind, j, last):
                at, n = (B - 1, 1) if last else (0, B - 1)
                return nc.vector.tensor_tensor(on[:, kind, j, :].rearrange("p (b c) -> p b c", b=B)[:, at:at + n, :],
                                               O[j][int(last)][:, :, kind * C:(kind + 1) * C],
                                               rs[:, j, at:at + n].unsqueeze(2).to_broadcast([P, n, C]), ALU.mult)

            dve.wait_ge(s["pv_mm"], B - 1)
            dve.wait_ge(s["rsum_ready"], 1)
            for j in range(J):
                normalise(1, j, last=False).then_inc(s["onu_ready"], 1)
            dve.wait_ge(s["pv0_mm"], 1)
            normalise(1, 0, last=True).then_inc(s["onu_ready"], 1)
            normalise(0, 0, last=False).then_inc(s["ono_ready"], 1)
            dve.wait_ge(s["pv_mm"], B)
            normalise(1, 1, last=True).then_inc(s["onu_ready"], 1)
            normalise(0, 0, last=True).then_inc(s["ono_ready"], 1)
            for last in (False, True):
                normalise(0, 1, last).then_inc(s["ono_ready"], 1)
            for j in range(J):
                dve.wait_ge(s["u_mm"], j + 1)
                nc.vector.bn_stats(ubst[:, j, :], U[:, j, :]).then_inc(s["ustats"], 1)
            dve.wait_ge(s["ustats"], J)
            nc.vector.bn_aggr(ubag[:, :], ubst[:, :, :].rearrange("p j s -> p (j s)")).then_inc(s["uagg"], 1)
            dve.wait_ge(s["uagg"], 1)
            nc.vector.scalar_tensor_tensor(ucen[:, :, :], U, ubag[:, 0:1],
                                           v["g_cbr"].unsqueeze(2).to_broadcast([P, J, P]),
                                           ALU.subtract, ALU.mult).then_inc(s["ucen_ready"], 1)
            dve.wait_ge(s["urstd"], 1)
            dve.wait_ge(s["ucen_ready"], 1)
            nc.vector.tensor_scalar(uaff[:, 0, :], ucen[:, 0, :], urstd[:, :],
                                    v["be_cbr"], ALU.mult, ALU.add).then_inc(s["uaff"], 1)
            dve.wait_ge(s["uaff"], 1)
            dve.wait_ge(s["o_mm"], 1)
            nc.vector.scalar_tensor_tensor(chunk(y, 0), uaff[:, 0, :], 0.0, chunk(OO, 0), ALU.max, ALU.add)\
                .then_inc(s["y_ready"], 1)
            dve.wait_ge(s["urelu"], 1)
            nc.vector.tensor_tensor(chunk(y, 1), uaff[:, 1, :], chunk(OO, 1), ALU.add).then_inc(s["y_ready"], 1)
            for j in range(J):
                dve.wait_ge(s["ysq_ready"], j + 1)
                if j == 0:
                    dve.wait_ge(s["ysq_eps"], 1)
                nc.vector.tensor_reduce(yvar[:, j, :], ysq[:, j, :, :], AX.X, ALU.add)\
                    .then_inc(s["yvar_ready"], 1)
            dve.wait_ge(s["yvar_ready"], J)
            nc.vector.reciprocal(yr2[:, :, :], yvar[:, :, :]).then_inc(s["yr2_ready"], 1)
            dve.wait_ge(s["yr2_ready"], 1)
            dve.wait_ge(s["ycs_ready"], J)
            for j in range(J):
                nc.vector.tensor_tensor(yw[:, j, :, :], YC[:, j, :, :],
                                        yr2[:, j, :].unsqueeze(2).to_broadcast([P, B, C]),
                                        ALU.mult).then_inc(s["yw_ready"], 1)
            dve.wait_ge(s["yrstd_ready"], 1)
            for j in range(J):
                nc.vector.tensor_tensor(xt[:, j, :, :], YC[:, j, :, :],
                                        yrstd[:, j, :].unsqueeze(2).to_broadcast([P, B, C]),
                                        ALU.mult).then_inc(s["xt_ready"], 1)
            dve.wait_ge(s["g_mm"], J)
            dve.wait_ge(s["cons_in"], 16)
            nc.vector.tensor_tensor(gbd[:, :], G, c["block"], ALU.mult).then_inc(s["g_ready"], 1)
            for j in range(J):
                dve.wait_ge(s["tsq_ready"], j + 1)
                nc.vector.tensor_copy(chunk(tcs, j), TC[j]).then_inc(s["tcs_ready"], 1)
            for j in range(J):
                dve.wait_ge(s["trstd_ready"], j + 1)
                if j == 0:
                    dve.wait_ge(s["raw_mm"], J)
                nc.vector.tensor_tensor(chunk(logit, j), chunk(RAW, j), chunk(trstd, j), ALU.mult)\
                    .then_inc(s["logits_ready"], 1)
            dve.wait_ge(s["logits_ready"], J)
            nc.vector.max(top[:, :], logit[:, :]).then_inc(s["top_ready"], 1)
            dve.wait_ge(s["top_ready"], 1)
            nc.vector.scalar_tensor_tensor(negmax[:, :], top[:, 0:1], v["gate_b"], v["gate_b"], ALU.add,
                                           ALU.subtract, reverse1=True).then_inc(s["negmax_ready"], 1)
            nc.vector.match_replace(taken[:, :], top[:, :], logit[:, :], TAKEN).then_inc(s["taken_ready"], 1)
            dve.wait_ge(s["gexp_ready"], 1)
            dve.wait_ge(s["taken_ready"], 1)
            for j in range(J):
                nc.vector.scalar_tensor_tensor(chunk(wm, j), chunk(taken, j), TAKEN, chunk(gexp, j),
                                               ALU.is_equal, ALU.mult).then_inc(s["wm_ready"], 1)
            dve.wait_ge(s["gsum_ready"], 1)
            nc.vector.reciprocal(grec[:, :], gsum[:, :]).then_inc(s["grec_ready"], 1)
            dve.wait_ge(s["wt_mm"], 1)
            nc.vector.tensor_copy(wt[:, 0, :, :].rearrange("p b e -> p (b e)"), WT[:, 0, :])\
                .then_inc(s["wt_dve"], 1)
            dve.wait_ge(s["pool_mm"], 1)
            dve.wait_ge(s["grec_ready"], 1)
            nc.vector.tensor_tensor(rep[:, :, :], POOL.unsqueeze(1).to_broadcast([P, GE, C]),
                                    grec[:, :].unsqueeze(2).to_broadcast([P, GE, C]),
                                    ALU.mult).then_inc(s["rep_ready"], 1)
            dve.wait_ge(s["rept_mm"], 1)
            dve.wait_ge(s["masks_in"], 16)
            nc.vector.tensor_tensor(pooled[:, :, :, :],
                                    REPT.rearrange("p (b e) -> p b e", b=B)[:, :, 0:E]
                                    .rearrange("p b (g e) -> p g e b", g=NG),
                                    msk[:, 0:E * B].rearrange("p (g e b) -> p g e b", g=NG, e=GE),
                                    ALU.mult).then_inc(s["pool_ready"], 1)
            nc.vector.tensor_tensor(place[:, :], msk[:, E * B:], grec[:, :].to_broadcast([P, GE]), ALU.mult)\
                .then_inc(s["place_ready"], 1)
            dve.wait_ge(s["z_mm"], 1)
            dve.wait_ge(s["place_ready"], 1)
            nc.vector.tensor_tensor(zsel[:, :, :], Z.rearrange("p (e c) -> p e c", e=GE),
                                    place[:, :].unsqueeze(2).to_broadcast([P, GE, C]),
                                    ALU.mult).then_inc(s["zsel_ready"], 1)
            dve.wait_ge(s["zsel_ready"], 1)
            nc.vector.tensor_reduce(zsum[:, :], zsel[:, :, :].rearrange("p e c -> p c e"), AX.X, ALU.add)\
                .then_inc(s["zsum_ready"], 1)
            dve.wait_ge(s["zsum_ready"], 1)
            nc.vector.tensor_tensor(zbd[:, :, :], zsum[:, :].unsqueeze(1).to_broadcast([P, B, C]),
                                    c["block"].rearrange("p (b c) -> p b c", b=B), ALU.mult)\
                .then_inc(s["z_ready"], 1)
            dve.wait_ge(s["f_mm"], 1)
            nc.vector.tensor_copy(fin[:, 0:P], T[:, 0, :]).then_inc(s["final_dve"], 1)

        @block.tensor
        def _(pe):
            mm = nc.tensor.matmul

            def keep_warm(n, at=3):
                for _ in range(n):
                    mm(bank(at, 2 * P), idle[:, 0:P], idle, start=True, stop=True)

            keep_warm(WARM["load"], at=0)
            pe.wait_ge(s["wvo_in"], 16)
            pe.wait_ge(s["x_in"], 16)
            mm(PROD1, m["woT"], m["wv"], start=True, stop=True).then_inc(s["prod1_mm"], 1)
            mm(VO, m["wv"], m["woT"], start=True, stop=True).then_inc(s["vmat0_mm"], 1)
            mm(BIAS1, m["woT"], v["bv"], start=True, stop=True).then_inc(s["bias1_mm"], 1)
            pe.wait_ge(s["prod1_ready"], 1)
            mm(PROD2, prod1[:, :], m["wcT"], start=True, stop=True).then_inc(s["prod2_mm"], 1)
            pe.wait_ge(s["xn_ready"], 1)
            pe.wait_ge(s["wqk_in"], 16)
            mm(KK, m["wkT"], xn[:, :], start=True, stop=True).then_inc(s["k_mm"], 1)
            mm(Q, m["wqT"], xn[:, :], start=True, stop=True).then_inc(s["q_mm"], 1)
            pe.wait_ge(s["prod2_ready"], 1)
            pe.wait_ge(s["vmat0_ready"], 1)
            for i in range(J):
                last = mm(V[:, i, :, :, :].rearrange("p k b c -> p (k b c)"), chunk(xn, i),
                          vmat[:, :, :].rearrange("p k c -> p (k c)"), start=True, stop=True)
            last.then_inc(s["v_mm"], 1)

            def scores(b):
                pe.wait_ge(s["q_ready"], b + 1)
                for j in range(J):
                    last = mm(bank(SCORES[b], N, j * N), chunk(qm[:, b, :], j), k[:, :], start=True, stop=True)
                last.then_inc(s["s_mm"], 1)

            def transposes(b):
                pe.wait_ge(s["exp_ready"], J * (b + 1))
                if b == 0:
                    pe.wait_ge(s["cons_in"], 16)
                for j in range(J):
                    for i in range(J):
                        last = nc.tensor.transpose(bank(PT[b], P, i * N + j * P), chunk(prob[:, b, j, :], i),
                                                   c["ident"])
                last.then_inc(s["pt_mm"], 1)

            def attend(b):
                if b < B - 1:
                    pe.wait_ge(s["pt_dve"], b + 1)
                    if b == 0:
                        pe.wait_ge(s["vo_ready"], 1)
                else:
                    pe.wait_ge(s["pt_act"], 1)
                for j in range(J):
                    for i in range(J):
                        last = mm(O[j][b // (B - 1)][:, b % (B - 1), :], chunk(pt[:, b, i, :], j), vt[:, i, b, :],
                                  start=(i == 0), stop=(i == J - 1))
                    if b == B - 1 and j == 0:
                        last.then_inc(s["pv0_mm"], 1)
                last.then_inc(s["pv_mm"], 1)

            def start_u(j):
                mm(U[:, j, :], m["wcT"], chunk(xres, j), start=True, stop=False, skip_group_check=True)

            pe.wait_ge(s["k_ready"], 1)
            scores(0)
            scores(1)
            pe.wait_ge(s["xres_ready"], 1)
            scores(2)
            start_u(0)
            transposes(0)
            scores(3)
            transposes(1)
            attend(0)
            transposes(2)
            attend(1)
            transposes(3)
            start_u(1)
            attend(2)
            attend(3)
            for j in range(J):
                pe.wait_ge(s["onu_ready"], J + j + 1)
                mm(U[:, j, :], on[:, 1, j, :], c["ident"], start=False, stop=True,
                   skip_group_check=True).then_inc(s["u_mm"], 1)
            mm(OO, c["ident"], xres[:, :], start=True, stop=False, skip_group_check=True)
            for j in range(J):
                pe.wait_ge(s["ono_ready"], 2 * (j + 1))
                last = mm(chunk(OO, j), on[:, 0, j, :], c["ident"], start=False, stop=True,
                          skip_group_check=True)
            last.then_inc(s["o_mm"], 1)
            keep_warm(WARM["y"], at=5)
            for j in range(J):
                pe.wait_ge(s["y_ready"], j + 1)
                mm(YC[:, j, :, :].rearrange("p b c -> p (b c)"), chunk(y, j), c["center"],
                   start=True, stop=True).then_inc(s["yc_mm"], 1)
            for j in range(J):
                mm(TC[j], c["center"], chunk(y, j), start=True, stop=False, skip_group_check=True)
            for j in range(J):
                mm(T[:, j, :], c["ident"], chunk(y, j), start=True, stop=False, skip_group_check=True)
            keep_warm(WARM["yw"], at=2)
            for j in range(J):
                pe.wait_ge(s["yw_ready"], j + 1)
                if j == 0:
                    pe.wait_ge(s["ycs_ready"], J)
                mm(G, ycs[:, j, :, :].rearrange("p b c -> p (b c)"), yw[:, j, :, :].rearrange("p b c -> p (b c)"),
                   start=(j == 0), stop=(j == J - 1)).then_inc(s["g_mm"], 1)
            for j in range(J):
                pe.wait_ge(s["xt_ready"], j + 1)
                nc.tensor.transpose(XC[j], xt[:, j, :, :].rearrange("p b c -> p (b c)"), c["ident"])\
                    .then_inc(s["xc_mm"], 1)
            mm(VAR[0], c["mean"], eps[:, :], start=True, stop=False, skip_group_check=True)
            pe.wait_ge(s["g_ready"], 1)
            for j in range(J):
                pe.wait_ge(s["xc_ready"], j + 1)
                mm(TC[j], gbd[:, :], chunk(xc, j), start=False, stop=True, skip_group_check=True)\
                    .then_inc(s["tc_mm"], 1)
            mm(VAR[1], c["mean"], eps[:, :], start=True, stop=False, skip_group_check=True)
            for j in range(J):
                pe.wait_ge(s["tsq_ready"], j + 1)
                mm(VAR[j], c["mean"], chunk(tsq, j), start=False, stop=True, skip_group_check=True)\
                    .then_inc(s["var_mm"], 1)
            for j in range(J):
                pe.wait_ge(s["tcs_ready"], j + 1)
                mm(chunk(RAW, j), c["gateT"], chunk(tcs, j), start=True, stop=True).then_inc(s["raw_mm"], 1)
            for j in range(J):
                mm(T[:, j, :], gbd[:, :], chunk(xc, j), start=False, stop=False, skip_group_check=True)
            pe.wait_ge(s["rows_in"], 16)
            mm(Z, row[:, 3, :], row[:, 1, 0:C].unsqueeze(1).to_broadcast([E, GE, C]), start=True,
               stop=False, skip_group_check=True)
            keep_warm(WARM["x2c"])
            pe.wait_ge(s["x2c_ready"], 1)
            for j in range(J):
                last = nc.tensor.transpose(chunk(X2T, j), chunk(x2c, j), c["ident"])
            last.then_inc(s["x2t_mm"], 1)
            pe.wait_ge(s["trstd_ready"], J)
            mm(HH[0], row[:, 0, :], row[:, 2, 0:E * B // 2], start=True, stop=False, skip_group_check=True)
            keep_warm(WARM["wm"])
            for j in range(J):
                pe.wait_ge(s["wm_ready"], j + 1)
                if j == 0:
                    pe.wait_ge(s["x2t_ready"], 1)
                nc.tensor.transpose(WT[:, j, :], chunk(wm, j), c["ident"]).then_inc(s["wt_mm"], 1)
            keep_warm(WARM["wt"])
            pe.wait_ge(s["wt_act"], 1)
            pe.wait_ge(s["wt_dve"], 1)
            for b in range(B):
                for j in range(J):
                    last = mm(img(POOL, b), wt[:, j, b, :], x2t[:, j, b, :], start=(j == 0), stop=(j == J - 1))
            last.then_inc(s["pool_mm"], 1)
            mm(HH[1], row[:, 0, :], row[:, 2, E * B // 2:E * B], start=True, stop=False, skip_group_check=True)
            keep_warm(WARM["rep"])
            pe.wait_ge(s["rep_ready"], 1)
            nc.tensor.transpose(REPT, rep[:, :, :].rearrange("p g c -> p (g c)"), c["ident"])\
                .then_inc(s["rept_mm"], 1)
            keep_warm(WARM["rep"])
            pe.wait_ge(s["pool_ready"], 1)
            pe.wait_ge(s["w1_in"], 16)
            for g in range(NG):
                half, at = g // (NG // 2), g % (NG // 2) * GE * B
                last = mm(HH[half][:, at:at + GE * B], w1s[:, g, :],
                          pooled[:, g, :, :].rearrange("p e b -> p (e b)"),
                          start=False, stop=True, skip_group_check=True)
                if g % (NG // 2) == NG // 2 - 1:
                    last.then_inc(s["h_mm"], 1)
            keep_warm(WARM["h"])
            for g in range(NG):
                pe.wait_ge(s["h_ready"], g // (NG // 2) + 1)
                if g == 0:
                    pe.wait_ge(s["w2_in"], 16)
                last = mm(Z, hdiag[:, g, :], w2s[:, g * GE:(g + 1) * GE, :].rearrange("p e c -> p (e c)"),
                          start=False, stop=(g == NG - 1), skip_group_check=True)
            last.then_inc(s["z_mm"], 1)
            keep_warm(WARM["z"])
            pe.wait_ge(s["z_ready"], 1)
            for j in range(J):
                mm(T[:, j, :], zbd[:, :, :].rearrange("p b c -> p (b c)"), chunk(wm, j),
                   start=False, stop=True, skip_group_check=True).then_inc(s["f_mm"], 1)


def kernel(**inputs):
    import concourse.bacc as bacc
    from concourse.bass_utils import run_bass_kernel_spmd

    a = {n: np.asarray(t) for n, t in inputs.items()}
    f = np.float32

    def tiled(t):
        return np.tile(t, B)

    def diagonal(t):
        d = np.zeros((B, C, B, t.shape[1]), f)
        for b in range(B):
            d[b, :, b, :] = t
        return d.reshape(P, -1)

    L = "L0_conv_"
    gate_b = np.zeros(EP, f)
    gate_b[:E] = a["L1_ffn_gate_b"]
    cols = [a[L + n] for n in VEC[:-1]] + [gate_b]
    vecs = np.stack([tiled(t) for t in cols], axis=1)

    gateT = np.zeros((C, EP), f)
    gateT[:, :E] = a["L1_ffn_gate_w"].T
    xv = np.concatenate([a["x"].reshape(P, N), vecs], axis=1)
    wqk = np.stack([diagonal(a[L + "wq"].T), diagonal(a[L + "wk"].T)], axis=1)
    mats = np.stack([diagonal(t) for t in (a[L + "wv"], a[L + "wo"].T, a[L + "w_cbr"].T)], axis=1)

    blk = diagonal(np.ones((C, C), f))
    cons = np.stack([np.eye(P, dtype=f), np.eye(P, dtype=f) - blk / f(C), blk / f(C), blk,
                     diagonal(gateT)], axis=1)
    masks = np.zeros((P, E * B + GE), f)
    masks[:, :E * B] = np.broadcast_to(np.eye(GE, dtype=f)[:, None, None, :, None],
                                     (GE, C, NG, GE, B)).reshape(P, E * B)
    for b in range(B):
        masks[b * EP:b * EP + E, E * B:] = np.tile(np.eye(GE, dtype=f), (NG, 1))

    w1, w2 = a["L1_ffn_weight1"], a["L1_ffn_weight2"]
    w1g = np.ascontiguousarray(w1[:, :C, :].reshape(NG, GE, C, H).transpose(1, 2, 0, 3).reshape(P, NG, H))
    w2g = np.ascontiguousarray(w2[:, :H, :].transpose(1, 0, 2))
    rows = np.zeros((E, 4, P), f)
    rows[:, 0, :] = w1[:, C, :]
    rows[:, 1, :C] = w2[:, H, :]
    rows[:, 2, :E * B] = np.repeat(np.eye(E, dtype=f), B, axis=1)
    for b in range(B):
        rows[:, 3, b * EP:b * EP + E] = np.eye(E, dtype=f)

    arrays = {"xv": xv, "wqk": wqk, "mats": mats,
              "bcb": np.tile(a[L + "b_cbr"], (P, B)), "cons": cons,
              "masks": masks, "w1": w1g, "w2": w2g, "rows": rows}
    nc = bacc.Bacc("TRN2", target_bir_lowering=False, num_devices=1)
    args = [nc.dram_tensor(n, t.shape, F32, kind="ExternalInput").ap() for n, t in arrays.items()]
    args.append(nc.dram_tensor("out", (P, N), F32, kind="ExternalOutput").ap())
    hybrid_block(nc, *args)
    r = run_bass_kernel_spmd(nc, [arrays], core_ids=[0])
    return r.results[0]["out"].reshape(B, C, 16, 16)
```
